# Optimizing a Trainium2 kernel written in Bass

```python
import numpy as np
import jax
import jax.numpy as jnp

def _softmax(x, axis=-1):
    return jax.nn.softmax(x, axis=axis)

def _gelu(x):
    return jax.nn.gelu(x, approximate=True)

def _silu(x):
    return jax.nn.silu(x)

def _sigmoid(x):
    return jax.nn.sigmoid(x)

def _layernorm(x, axis=-1, eps=1e-05):
    m = jnp.mean(x, axis=axis, keepdims=True)
    v = jnp.var(x, axis=axis, keepdims=True)
    return (x - m) / jnp.sqrt(v + eps)

def _scatter_add(tgt, idx, src, axis=0):
    return tgt.at[idx].add(src)

def _segment_sum(src, seg, n):
    return jax.ops.segment_sum(src, seg, n)
kernel_name = 'mk_seq_preln_d2_jaxref_r8_25b8b1'

def setup_inputs(seed: int=0):
    np.random.seed(seed)
    _w = jnp.asarray

    def _L0_attn_setup():
        import jax, jax.numpy as jnp
        import numpy as np
        B, S, D, H = (4, 256, 128, 512)
        EPS = 1e-12

        def _linear(x, W, b):
            return x @ W.T + b
        key = jax.random.key(seed)
        ks = jax.random.split(key, 14)
        s = lambda d: 1.0 / np.sqrt(d)
        return {'x': jax.random.normal(ks[0], (B, S, D), dtype=jnp.float32), 'Wq': jax.random.normal(ks[1], (D, D), dtype=jnp.float32) * s(D), 'bq': jax.random.normal(ks[2], (D,), dtype=jnp.float32) * 0.01, 'Wk': jax.random.normal(ks[3], (D, D), dtype=jnp.float32) * s(D), 'bk': jax.random.normal(ks[4], (D,), dtype=jnp.float32) * 0.01, 'Wv': jax.random.normal(ks[5], (D, D), dtype=jnp.float32) * s(D), 'bv': jax.random.normal(ks[6], (D,), dtype=jnp.float32) * 0.01, 'W1': jax.random.normal(ks[7], (D, D), dtype=jnp.float32) * s(D), 'b1': jax.random.normal(ks[8], (D,), dtype=jnp.float32) * 0.01, 'W2': jax.random.normal(ks[9], (H, D), dtype=jnp.float32) * s(D), 'b2': jax.random.normal(ks[10], (H,), dtype=jnp.float32) * 0.01, 'W3': jax.random.normal(ks[11], (D, H), dtype=jnp.float32) * s(H), 'b3': jax.random.normal(ks[12], (D,), dtype=jnp.float32) * 0.01}
    _L0_attn_in = _L0_attn_setup()

    def _L0_ffn_setup():
        import jax, jax.numpy as jnp
        import numpy as np
        DIM = 128

        def _reference_tuple_inner(x, W_r, W_k, W_v, mu_r, mu_k):
            B, T, C = x.shape
            x_prev = jnp.concatenate([jnp.zeros((B, 1, C), x.dtype), x[:, :-1, :]], axis=1)
            xr = mu_r * x + (1.0 - mu_r) * x_prev
            xk = mu_k * x + (1.0 - mu_k) * x_prev
            r = jax.nn.sigmoid(jnp.einsum('btc,dc->btd', xr, W_r))
            k = jnp.einsum('btc,dc->btd', xk, W_k)
            k_act = jnp.square(jax.nn.relu(k))
            out = r * jnp.einsum('btc,dc->btd', k_act, W_v)
            new_state = x[:, -1, :]
            return (out, new_state)
        key = jax.random.key(seed)
        ks = jax.random.split(key, 6)
        B, T, C = (8, 256, DIM)
        x = jax.random.normal(ks[0], (B, T, C), dtype=jnp.float32)
        s = 1.0 / np.sqrt(C)
        W_r = jax.random.uniform(ks[1], (C, C), jnp.float32, -s, s)
        W_k = jax.random.uniform(ks[2], (C, C), jnp.float32, -s, s)
        W_v = jax.random.uniform(ks[3], (C, C), jnp.float32, -s, s)
        mu_r = jax.random.uniform(ks[4], (C,), jnp.float32)
        mu_k = jax.random.uniform(ks[5], (C,), jnp.float32)
        return {'x': x, 'W_r': W_r, 'W_k': W_k, 'W_v': W_v, 'mu_r': mu_r, 'mu_k': mu_k}
    _L0_ffn_in = _L0_ffn_setup()

    def _L1_attn_setup():
        import jax, jax.numpy as jnp
        import numpy as np
        DIM = 128
        HEADS = 16
        HD = DIM // HEADS
        B, S = (4, 512)
        LEVELS = 3
        HID = 4 * DIM
        CHUNK = 128
        EPS = 1e-05

        def layernorm(x, g, b):
            m = jnp.mean(x, axis=-1, keepdims=True)
            v = jnp.var(x, axis=-1, keepdims=True)
            return (x - m) * jax.lax.rsqrt(v + EPS) * g + b

        def _linear_attn_with_memory(h, wq, wk, wv, wo):
            b, s, d = h.shape

            def heads(w):
                return (h @ w).reshape(b, s, HEADS, HD).transpose(0, 2, 1, 3)
            q, k, v = (heads(wq), heads(wk), heads(wv))
            nc = s // CHUNK

            def to_chunks(a):
                return a.reshape(b, HEADS, nc, CHUNK, HD).transpose(2, 0, 1, 3, 4)
            mask = jnp.tril(jnp.ones((CHUNK, CHUNK), h.dtype))

            def step(M, qkv):
                qc, kc, vc = qkv
                inter = jnp.einsum('bhvk,bhck->bhcv', M, qc)
                scores = jnp.einsum('bhcd,bhed->bhce', qc, kc) * mask
                intra = jnp.einsum('bhce,bhev->bhcv', scores, vc)
                M_new = M + jnp.einsum('bhcv,bhck->bhvk', vc, kc)
                return (M_new, inter + intra)
            M0 = jnp.zeros((b, HEADS, HD, HD), h.dtype)
            _, ys = jax.lax.scan(step, M0, (to_chunks(q), to_chunks(k), to_chunks(v)))
            y = ys.transpose(1, 2, 0, 3, 4).reshape(b, HEADS, s, HD)
            y = y.transpose(0, 2, 1, 3).reshape(b, s, d)
            return y @ wo
        key = jax.random.key(seed)
        ks = jax.random.split(key, 10)
        std = 0.02
        return {'x': jax.random.normal(ks[0], (B, S, DIM), jnp.float32), 'ln1_g': jnp.ones((DIM,), jnp.float32), 'ln1_b': jnp.zeros((DIM,), jnp.float32), 'wq': jax.random.normal(ks[1], (DIM, DIM), jnp.float32) * std, 'wk': jax.random.normal(ks[2], (DIM, DIM), jnp.float32) * std, 'wv': jax.random.normal(ks[3], (DIM, DIM), jnp.float32) * std, 'wo': jax.random.normal(ks[4], (DIM, DIM), jnp.float32) * std, 'ln2_g': jnp.ones((DIM,), jnp.float32), 'ln2_b': jnp.zeros((DIM,), jnp.float32), 'cms_w1': jax.random.normal(ks[5], (LEVELS, DIM, HID), jnp.float32) * std, 'cms_b1': jnp.zeros((LEVELS, HID), jnp.float32), 'cms_w2': jax.random.normal(ks[6], (LEVELS, HID, DIM), jnp.float32) * std, 'cms_b2': jnp.zeros((LEVELS, DIM), jnp.float32)}
    _L1_attn_in = _L1_attn_setup()

    def _L1_ffn_setup():
        import jax, jax.numpy as jnp
        import numpy as np
        B, N, D = (4, 512, 128)
        E, K, H, ITERS = (8, 2, 64, 2)
        DT = 0.1
        C = 2 * D

        def _gelu(x):
            return jax.nn.gelu(x, approximate=False)

        def _inl(ctrl, xs, vs, mu):
            a, b, g = jnp.split(ctrl, 3, axis=-1)
            v_next = jax.nn.sigmoid(a) * vs - jax.nn.softplus(b) * (xs - mu)
            x_next = xs + DT * jax.nn.sigmoid(g) * v_next
            return (x_next, v_next)

        def _experts(ctx, idx, w1, b1, w2, b2):
            out = jnp.zeros((ctx.shape[0], w2.shape[2]), ctx.dtype)
            for e in range(E):
                h = _gelu(ctx @ w1[e] + b1[e])
                o = h @ w2[e] + b2[e]
                out = out + jnp.where((idx == e)[:, None], o, jnp.float32(0))
            return out

        def _forward(x, integration_weight, mu, router_w1, router_b1, router_w2, router_b2, halt_w1, halt_b1, halt_w2, halt_b2, expert_w1, expert_b1, expert_w2, expert_b2, shared_w1, shared_b1, shared_w2, shared_b2, shared_weight, refine_w1, refine_b1, refine_w2, refine_b2):
            b, n, d = x.shape
            xf = x.reshape(b * n, d)
            logits = _gelu(xf @ router_w1 + router_b1) @ router_w2 + router_b2
            probs = jax.nn.softmax(logits, axis=-1)
            topk_p, topk_i = jax.lax.top_k(probs, K)
            topk_p = topk_p / jnp.sum(topk_p, axis=-1, keepdims=True)
            flat_idx = topk_i.reshape(-1)
            flat_w = topk_p.reshape(-1, 1)
            v = jnp.zeros_like(xf)
            integrated = xf
            for _ in range(ITERS):
                ctx = jnp.concatenate([integrated, v], axis=-1)
                shared_ctrl = _gelu(ctx @ shared_w1 + shared_b1) @ shared_w2 + shared_b2
                x_sh, v_sh = _inl(shared_ctrl, integrated, v, mu)
                sw = jax.nn.sigmoid(shared_weight)
                ctx_e = jnp.repeat(ctx, K, axis=0)
                x_e = jnp.repeat(integrated, K, axis=0)
                v_e = jnp.repeat(v, K, axis=0)
                ctrl = _experts(ctx_e, flat_idx, expert_w1, expert_b1, expert_w2, expert_b2)
                x_r, v_r = _inl(ctrl, x_e, v_e, mu)
                x_r = (x_r * flat_w).reshape(-1, K, d).sum(axis=1)
                v_r = (v_r * flat_w).reshape(-1, K, d).sum(axis=1)
                x_next = sw * x_sh + (1.0 - sw) * x_r
                v_next = sw * v_sh + (1.0 - sw) * v_r
                halt = jax.nn.sigmoid(_gelu(integrated @ halt_w1 + halt_b1) @ halt_w2 + halt_b2)
                integrated = integrated + halt * (x_next - integrated)
                v = v + halt * (v_next - v)
            refined = _gelu(integrated @ refine_w1 + refine_b1) @ refine_w2 + refine_b2
            out = xf + integration_weight * refined
            return out.reshape(b, n, d)
        key = jax.random.key(seed)
        ks = jax.random.split(key, 12)
        rn = lambda k, s, sc=0.02: jax.random.normal(k, s, dtype=jnp.float32) * sc
        z = lambda s: jnp.zeros(s, jnp.float32)
        return {'x': jax.random.normal(ks[0], (B, N, D), dtype=jnp.float32), 'integration_weight': jnp.full((D,), 0.5, jnp.float32), 'mu': z((D,)), 'router_w1': rn(ks[1], (D, D // 4)), 'router_b1': z((D // 4,)), 'router_w2': rn(ks[2], (D // 4, E)), 'router_b2': z((E,)), 'halt_w1': rn(ks[3], (D, D // 4)), 'halt_b1': z((D // 4,)), 'halt_w2': rn(ks[4], (D // 4, 1)), 'halt_b2': z((1,)), 'expert_w1': rn(ks[5], (E, C, H)), 'expert_b1': z((E, H)), 'expert_w2': rn(ks[6], (E, H, 3 * D)), 'expert_b2': z((E, 3 * D)), 'shared_w1': rn(ks[7], (C, H)), 'shared_b1': z((H,)), 'shared_w2': rn(ks[8], (H, 3 * D)), 'shared_b2': z((3 * D,)), 'shared_weight': jnp.float32(0.5), 'refine_w1': rn(ks[9], (D, 2 * D)), 'refine_b1': z((2 * D,)), 'refine_w2': rn(ks[10], (2 * D, D)), 'refine_b2': z((D,))}
    _L1_ffn_in = _L1_ffn_setup()
    _d = {'L0_attn_x': _L0_attn_in['x'], 'L0_attn_Wq': _L0_attn_in['Wq'], 'L0_attn_bq': _L0_attn_in['bq'], 'L0_attn_Wk': _L0_attn_in['Wk'], 'L0_attn_bk': _L0_attn_in['bk'], 'L0_attn_Wv': _L0_attn_in['Wv'], 'L0_attn_bv': _L0_attn_in['bv'], 'L0_attn_W1': _L0_attn_in['W1'], 'L0_attn_b1': _L0_attn_in['b1'], 'L0_attn_W2': _L0_attn_in['W2'], 'L0_attn_b2': _L0_attn_in['b2'], 'L0_attn_W3': _L0_attn_in['W3'], 'L0_attn_b3': _L0_attn_in['b3'], 'L0_ffn_W_r': _L0_ffn_in['W_r'], 'L0_ffn_W_k': _L0_ffn_in['W_k'], 'L0_ffn_W_v': _L0_ffn_in['W_v'], 'L0_ffn_mu_r': _L0_ffn_in['mu_r'], 'L0_ffn_mu_k': _L0_ffn_in['mu_k'], 'L1_attn_ln1_g': _L1_attn_in['ln1_g'], 'L1_attn_ln1_b': _L1_attn_in['ln1_b'], 'L1_attn_wq': _L1_attn_in['wq'], 'L1_attn_wk': _L1_attn_in['wk'], 'L1_attn_wv': _L1_attn_in['wv'], 'L1_attn_wo': _L1_attn_in['wo'], 'L1_attn_ln2_g': _L1_attn_in['ln2_g'], 'L1_attn_ln2_b': _L1_attn_in['ln2_b'], 'L1_attn_cms_w1': _L1_attn_in['cms_w1'], 'L1_attn_cms_b1': _L1_attn_in['cms_b1'], 'L1_attn_cms_w2': _L1_attn_in['cms_w2'], 'L1_attn_cms_b2': _L1_attn_in['cms_b2'], 'L1_ffn_integration_weight': _L1_ffn_in['integration_weight'], 'L1_ffn_mu': _L1_ffn_in['mu'], 'L1_ffn_router_w1': _L1_ffn_in['router_w1'], 'L1_ffn_router_b1': _L1_ffn_in['router_b1'], 'L1_ffn_router_w2': _L1_ffn_in['router_w2'], 'L1_ffn_router_b2': _L1_ffn_in['router_b2'], 'L1_ffn_halt_w1': _L1_ffn_in['halt_w1'], 'L1_ffn_halt_b1': _L1_ffn_in['halt_b1'], 'L1_ffn_halt_w2': _L1_ffn_in['halt_w2'], 'L1_ffn_halt_b2': _L1_ffn_in['halt_b2'], 'L1_ffn_expert_w1': _L1_ffn_in['expert_w1'], 'L1_ffn_expert_b1': _L1_ffn_in['expert_b1'], 'L1_ffn_expert_w2': _L1_ffn_in['expert_w2'], 'L1_ffn_expert_b2': _L1_ffn_in['expert_b2'], 'L1_ffn_shared_w1': _L1_ffn_in['shared_w1'], 'L1_ffn_shared_b1': _L1_ffn_in['shared_b1'], 'L1_ffn_shared_w2': _L1_ffn_in['shared_w2'], 'L1_ffn_shared_b2': _L1_ffn_in['shared_b2'], 'L1_ffn_shared_weight': _L1_ffn_in['shared_weight'], 'L1_ffn_refine_w1': _L1_ffn_in['refine_w1'], 'L1_ffn_refine_b1': _L1_ffn_in['refine_b1'], 'L1_ffn_refine_w2': _L1_ffn_in['refine_w2'], 'L1_ffn_refine_b2': _L1_ffn_in['refine_b2']}
    _x0 = _d['L0_attn_x']
    _d['L0_attn_x'] = jax.random.normal(jax.random.fold_in(jax.random.key(seed), 1), (8, 512, 128), dtype=_x0.dtype)
    del _x0
    return _d

def reference(L0_attn_x, L0_attn_Wq, L0_attn_bq, L0_attn_Wk, L0_attn_bk, L0_attn_Wv, L0_attn_bv, L0_attn_W1, L0_attn_b1, L0_attn_W2, L0_attn_b2, L0_attn_W3, L0_attn_b3, L0_ffn_W_r, L0_ffn_W_k, L0_ffn_W_v, L0_ffn_mu_r, L0_ffn_mu_k, L1_attn_ln1_g, L1_attn_ln1_b, L1_attn_wq, L1_attn_wk, L1_attn_wv, L1_attn_wo, L1_attn_ln2_g, L1_attn_ln2_b, L1_attn_cms_w1, L1_attn_cms_b1, L1_attn_cms_w2, L1_attn_cms_b2, L1_ffn_integration_weight, L1_ffn_mu, L1_ffn_router_w1, L1_ffn_router_b1, L1_ffn_router_w2, L1_ffn_router_b2, L1_ffn_halt_w1, L1_ffn_halt_b1, L1_ffn_halt_w2, L1_ffn_halt_b2, L1_ffn_expert_w1, L1_ffn_expert_b1, L1_ffn_expert_w2, L1_ffn_expert_b2, L1_ffn_shared_w1, L1_ffn_shared_b1, L1_ffn_shared_w2, L1_ffn_shared_b2, L1_ffn_shared_weight, L1_ffn_refine_w1, L1_ffn_refine_b1, L1_ffn_refine_w2, L1_ffn_refine_b2):

    def _L0_attn_ref(x, Wq, bq, Wk, bk, Wv, bv, W1, b1, W2, b2, W3, b3):
        import jax, jax.numpy as jnp
        import numpy as np
        B, S, D, H = (4, 256, 128, 512)
        EPS = 1e-12

        def _linear(x, W, b):
            return x @ W.T + b
        Q = _linear(x, Wq, bq)
        K = _linear(x, Wk, bk)
        V = _linear(x, Wv, bv)
        Q = Q / jnp.maximum(jnp.linalg.norm(Q, axis=2, keepdims=True), EPS)
        K = K / jnp.maximum(jnp.linalg.norm(K, axis=2, keepdims=True), EPS)
        sim = jnp.einsum('bqd,bkd->bqk', Q, K)
        attn = jax.nn.softmax(sim, axis=2)
        out = jnp.einsum('bqk,bkd->bqd', attn, V)
        h = jax.nn.relu(_linear(out, W1, b1))
        h = jax.nn.relu(_linear(h, W2, b2))
        return _linear(h, W3, b3)

    def _L0_ffn_ref(x, W_r, W_k, W_v, mu_r, mu_k):
        import jax, jax.numpy as jnp
        import numpy as np
        DIM = 128

        def _reference_tuple_inner(x, W_r, W_k, W_v, mu_r, mu_k):
            B, T, C = x.shape
            x_prev = jnp.concatenate([jnp.zeros((B, 1, C), x.dtype), x[:, :-1, :]], axis=1)
            xr = mu_r * x + (1.0 - mu_r) * x_prev
            xk = mu_k * x + (1.0 - mu_k) * x_prev
            r = jax.nn.sigmoid(jnp.einsum('btc,dc->btd', xr, W_r))
            k = jnp.einsum('btc,dc->btd', xk, W_k)
            k_act = jnp.square(jax.nn.relu(k))
            out = r * jnp.einsum('btc,dc->btd', k_act, W_v)
            new_state = x[:, -1, :]
            return (out, new_state)
        return _reference_tuple_inner(x, W_r, W_k, W_v, mu_r, mu_k)[0]

    def _L1_attn_ref(x, ln1_g, ln1_b, wq, wk, wv, wo, ln2_g, ln2_b, cms_w1, cms_b1, cms_w2, cms_b2):
        import jax, jax.numpy as jnp
        import numpy as np
        DIM = 128
        HEADS = 16
        HD = DIM // HEADS
        B, S = (4, 512)
        LEVELS = 3
        HID = 4 * DIM
        CHUNK = 128
        EPS = 1e-05

        def layernorm(x, g, b):
            m = jnp.mean(x, axis=-1, keepdims=True)
            v = jnp.var(x, axis=-1, keepdims=True)
            return (x - m) * jax.lax.rsqrt(v + EPS) * g + b

        def _linear_attn_with_memory(h, wq, wk, wv, wo):
            b, s, d = h.shape

            def heads(w):
                return (h @ w).reshape(b, s, HEADS, HD).transpose(0, 2, 1, 3)
            q, k, v = (heads(wq), heads(wk), heads(wv))
            nc = s // CHUNK

            def to_chunks(a):
                return a.reshape(b, HEADS, nc, CHUNK, HD).transpose(2, 0, 1, 3, 4)
            mask = jnp.tril(jnp.ones((CHUNK, CHUNK), h.dtype))

            def step(M, qkv):
                qc, kc, vc = qkv
                inter = jnp.einsum('bhvk,bhck->bhcv', M, qc)
                scores = jnp.einsum('bhcd,bhed->bhce', qc, kc) * mask
                intra = jnp.einsum('bhce,bhev->bhcv', scores, vc)
                M_new = M + jnp.einsum('bhcv,bhck->bhvk', vc, kc)
                return (M_new, inter + intra)
            M0 = jnp.zeros((b, HEADS, HD, HD), h.dtype)
            _, ys = jax.lax.scan(step, M0, (to_chunks(q), to_chunks(k), to_chunks(v)))
            y = ys.transpose(1, 2, 0, 3, 4).reshape(b, HEADS, s, HD)
            y = y.transpose(0, 2, 1, 3).reshape(b, s, d)
            return y @ wo
        x = x + _linear_attn_with_memory(layernorm(x, ln1_g, ln1_b), wq, wk, wv, wo)
        h = layernorm(x, ln2_g, ln2_b)
        for l in range(LEVELS):
            h = jax.nn.gelu(h @ cms_w1[l] + cms_b1[l]) @ cms_w2[l] + cms_b2[l]
        return x + h

    def _L1_ffn_ref(x, integration_weight, mu, router_w1, router_b1, router_w2, router_b2, halt_w1, halt_b1, halt_w2, halt_b2, expert_w1, expert_b1, expert_w2, expert_b2, shared_w1, shared_b1, shared_w2, shared_b2, shared_weight, refine_w1, refine_b1, refine_w2, refine_b2):
        import jax, jax.numpy as jnp
        import numpy as np
        B, N, D = (4, 512, 128)
        E, K, H, ITERS = (8, 2, 64, 2)
        DT = 0.1
        C = 2 * D

        def _gelu(x):
            return jax.nn.gelu(x, approximate=False)

        def _inl(ctrl, xs, vs, mu):
            a, b, g = jnp.split(ctrl, 3, axis=-1)
            v_next = jax.nn.sigmoid(a) * vs - jax.nn.softplus(b) * (xs - mu)
            x_next = xs + DT * jax.nn.sigmoid(g) * v_next
            return (x_next, v_next)

        def _experts(ctx, idx, w1, b1, w2, b2):
            out = jnp.zeros((ctx.shape[0], w2.shape[2]), ctx.dtype)
            for e in range(E):
                h = _gelu(ctx @ w1[e] + b1[e])
                o = h @ w2[e] + b2[e]
                out = out + jnp.where((idx == e)[:, None], o, jnp.float32(0))
            return out

        def _forward(x, integration_weight, mu, router_w1, router_b1, router_w2, router_b2, halt_w1, halt_b1, halt_w2, halt_b2, expert_w1, expert_b1, expert_w2, expert_b2, shared_w1, shared_b1, shared_w2, shared_b2, shared_weight, refine_w1, refine_b1, refine_w2, refine_b2):
            b, n, d = x.shape
            xf = x.reshape(b * n, d)
            logits = _gelu(xf @ router_w1 + router_b1) @ router_w2 + router_b2
            probs = jax.nn.softmax(logits, axis=-1)
            topk_p, topk_i = jax.lax.top_k(probs, K)
            topk_p = topk_p / jnp.sum(topk_p, axis=-1, keepdims=True)
            flat_idx = topk_i.reshape(-1)
            flat_w = topk_p.reshape(-1, 1)
            v = jnp.zeros_like(xf)
            integrated = xf
            for _ in range(ITERS):
                ctx = jnp.concatenate([integrated, v], axis=-1)
                shared_ctrl = _gelu(ctx @ shared_w1 + shared_b1) @ shared_w2 + shared_b2
                x_sh, v_sh = _inl(shared_ctrl, integrated, v, mu)
                sw = jax.nn.sigmoid(shared_weight)
                ctx_e = jnp.repeat(ctx, K, axis=0)
                x_e = jnp.repeat(integrated, K, axis=0)
                v_e = jnp.repeat(v, K, axis=0)
                ctrl = _experts(ctx_e, flat_idx, expert_w1, expert_b1, expert_w2, expert_b2)
                x_r, v_r = _inl(ctrl, x_e, v_e, mu)
                x_r = (x_r * flat_w).reshape(-1, K, d).sum(axis=1)
                v_r = (v_r * flat_w).reshape(-1, K, d).sum(axis=1)
                x_next = sw * x_sh + (1.0 - sw) * x_r
                v_next = sw * v_sh + (1.0 - sw) * v_r
                halt = jax.nn.sigmoid(_gelu(integrated @ halt_w1 + halt_b1) @ halt_w2 + halt_b2)
                integrated = integrated + halt * (x_next - integrated)
                v = v + halt * (v_next - v)
            refined = _gelu(integrated @ refine_w1 + refine_b1) @ refine_w2 + refine_b2
            out = xf + integration_weight * refined
            return out.reshape(b, n, d)
        return _forward(x, integration_weight, mu, router_w1, router_b1, router_w2, router_b2, halt_w1, halt_b1, halt_w2, halt_b2, expert_w1, expert_b1, expert_w2, expert_b2, shared_w1, shared_b1, shared_w2, shared_b2, shared_weight, refine_w1, refine_b1, refine_w2, refine_b2)
    x = L0_attn_x
    x = x + _L0_attn_ref(_layernorm(x, axis=-1), L0_attn_Wq, L0_attn_bq, L0_attn_Wk, L0_attn_bk, L0_attn_Wv, L0_attn_bv, L0_attn_W1, L0_attn_b1, L0_attn_W2, L0_attn_b2, L0_attn_W3, L0_attn_b3)
    x = x + _L0_ffn_ref(_layernorm(x, axis=-1), L0_ffn_W_r, L0_ffn_W_k, L0_ffn_W_v, L0_ffn_mu_r, L0_ffn_mu_k)
    x = x + _L1_attn_ref(_layernorm(x, axis=-1), L1_attn_ln1_g, L1_attn_ln1_b, L1_attn_wq, L1_attn_wk, L1_attn_wv, L1_attn_wo, L1_attn_ln2_g, L1_attn_ln2_b, L1_attn_cms_w1, L1_attn_cms_b1, L1_attn_cms_w2, L1_attn_cms_b2)
    x = x + _L1_ffn_ref(_layernorm(x, axis=-1), L1_ffn_integration_weight, L1_ffn_mu, L1_ffn_router_w1, L1_ffn_router_b1, L1_ffn_router_w2, L1_ffn_router_b2, L1_ffn_halt_w1, L1_ffn_halt_b1, L1_ffn_halt_w2, L1_ffn_halt_b2, L1_ffn_expert_w1, L1_ffn_expert_b1, L1_ffn_expert_w2, L1_ffn_expert_b2, L1_ffn_shared_w1, L1_ffn_shared_b1, L1_ffn_shared_w2, L1_ffn_shared_b2, L1_ffn_shared_weight, L1_ffn_refine_w1, L1_ffn_refine_b1, L1_ffn_refine_w2, L1_ffn_refine_b2)
    return x

_drawn_inputs = setup_inputs


def setup_inputs(seed=0):
    import zlib

    import numpy as np

    out = dict(_drawn_inputs(seed))
    spreads = {'L1_attn_ln1_g': (1.0, 0.2),
     'L1_attn_ln1_b': (0.0, 0.488),
     'L1_attn_ln2_g': (1.0, 0.6),
     'L1_attn_ln2_b': (0.0, 0.8),
     'L1_attn_cms_b1': (0.0, 0.669),
     'L1_attn_cms_b2': (0.0, 0.1),
     'L1_ffn_integration_weight': (0.5, 0.6),
     'L1_ffn_mu': (0.0, 0.8),
     'L1_ffn_router_b1': (0.0, 0.8),
     'L1_ffn_router_b2': (0.0, 0.8),
     'L1_ffn_halt_b1': (0.0, 0.8),
     'L1_ffn_expert_b1': (0.0, 0.8),
     'L1_ffn_expert_b2': (0.0, 0.8),
     'L1_ffn_shared_b1': (0.0, 0.8),
     'L1_ffn_shared_b2': (0.0, 0.8),
     'L1_ffn_refine_b1': (0.0, 0.8),
     'L1_ffn_refine_b2': (0.0, 0.439)}
    factors = {'L0_attn_Wq': 8.0,
     'L0_attn_bq': 8.0,
     'L0_attn_Wk': 8.0,
     'L0_attn_bk': 8.0,
     'L0_attn_Wv': 3.62,
     'L0_attn_bv': 8.0,
     'L0_attn_W1': 3.491,
     'L0_attn_b1': 8.0,
     'L0_attn_W2': 3.288,
     'L0_attn_b2': 7.745,
     'L0_attn_b3': 6.007,
     'L0_ffn_W_r': 3.116,
     'L0_ffn_mu_r': 6.131,
     'L1_attn_cms_w1': 8.0,
     'L1_attn_cms_w2': 4.711,
     'L1_ffn_router_w1': 8.0,
     'L1_ffn_router_w2': 8.0,
     'L1_ffn_halt_w1': 8.0,
     'L1_ffn_halt_w2': 8.0,
     'L1_ffn_expert_w1': 8.0,
     'L1_ffn_expert_w2': 8.0,
     'L1_ffn_shared_w1': 8.0,
     'L1_ffn_shared_w2': 8.0,
     'L1_ffn_refine_w1': 8.0,
     'L1_ffn_refine_w2': 8.0}
    for name, (base, spread) in spreads.items():
        noise = np.random.default_rng([zlib.crc32(name.encode()), seed]).standard_normal(out[name].shape)
        drawn = base * np.exp(spread * noise) if base else spread * noise
        out[name] = jnp.asarray(drawn.astype(out[name].dtype))
    for name, factor in factors.items():
        out[name] = (out[name] * factor).astype(out[name].dtype)
    return out
```

```python
import numpy as np
import concourse.bass as bass
from concourse import mybir
from contextlib import ExitStack

F32 = mybir.dt.float32
BF16 = mybir.dt.bfloat16
U32 = mybir.dt.uint32
ALU = mybir.AluOpType
ACT = mybir.ActivationFunctionType
AXX = mybir.AxisListType.X

P = 128
SEQ = 512
NSEQ = 8
TILES = SEQ // P
NT = NSEQ * TILES
HEADS, HD = 16, 8
LEVELS = 3
HC = 4
EXPERTS = 8
EHID = 64
HHID = 32
LN_EPS = 1e-5
NORM_EPS = 1e-12

EARLY = [
    ("ident", 128), ("tril", 128), ("blockdiag", 128),
    ("wqkv", 384), ("bqkv", 384), ("w1", 128), ("b1", 1), ("w2", 512), ("b2", 4), ("w3", 512), ("b3", 128),
    ("wr", 128), ("wk", 128), ("wv", 128), ("mu_r", 1), ("mu_k", 1),
    ("ln1_g", 1), ("ln1_b", 1), ("lqkv", 384), ("lwo", 128), ("ln2_g", 1), ("ln2_b", 1),
    ("cw1", LEVELS * 512), ("cb1", LEVELS * 4), ("cw2", LEVELS * 512), ("cb2", LEVELS), ("cb2row", 128),
]
LATE = [
    ("lident", 128), ("iota", 8),
    ("g1x", 96), ("g1v", 96), ("g1b", 1), ("ew1x", 512), ("ew1v", 512), ("eb1", 4),
    ("rw1", 128), ("rb1", 1), ("rw2", 8), ("rb2", 8),
    ("sw2", 384), ("hw2", 128), ("hb2", 1), ("ew2", 4 * 384), ("eb2", 384), ("sb2", 384),
    ("mu", 1), ("shw", 1), ("esel", 512),
    ("fw1", 256), ("fb1", 2), ("fw2", 256), ("fb2row", 128), ("iwrow", 128),
]


def columns(table):
    at, out = 0, {}
    for name, n in table:
        out[name] = (at, at + n)
        at += n
    return out, at


EARLY_AT, EARLY_N = columns(EARLY)
LATE_AT, LATE_N = columns(LATE)

SEMAPHORES = """
w_early w_late x_in0 x_in1 x_in2 x_in3 x_in4 x_in5 x_in6 x_in7 out_done
st_a0 st_b0 st_a1 st_b1 st_a2 st_b2 st_a3 st_b3 st_a4 st_b4 st_c ln_var ln_sd ln_rs
a1_xc a1_xn a1_tr a1_xt a1_mm a1_ev a1_sq a1_nrm a1_max a1_rn
a2_qk a2_xb a2_tq a2_tk a2_qT a2_kT a2_s a2_E a2_o a2_rc a2_on a2_to a2_oT a2_w1 a2_h1 a2_w2 a2_h2 a2_w3 a2_x
b_om b_xc b_xn b_tr b_xT b_tk b_xr b_xk b_r b_k b_rs b_kr b_ka b_o b_ot b_x
c1_x1 c1_hn c1_tr c1_hT c1_mm c1_tok c1_q c1_qT c1_m c1_M c1_kv c1_in c1_qm c1_red c1_yin c1_y c1_ty c1_yT c1_wo c1_xp
c3_xc c3_xn c3_xa c3_xb c3_tr c3_hT c3_w1 c3_g c3_w2 c3_w2e
k_sw k_dve k_sets k_iw
d0_xc d0_xn d0_xa d0_xb d0_tr d0_xi d0_r d0_rh d0_l d0_lg d0_mx d0_ix d0_if d0_oh d0_d d0_th d0_cw d0_wide d0_ot d0_ohT d0_ct d0_C
""".split() + [f"d_{n}" for n in
                "g ge m hm u ev ex ln sp xm t1 t2 vn U gU Va Vs Da Ds hv hx v v2 x".split()] + \
    "e_1 e_g e_2 e_t e_x".split()


UNITS = {
    1: [("b", 0, 4), ("b", 1, 5), ("b", 2, 6), ("g", 0, 7), ("g", 1, 4), ("g", 2, 5), ("h", 0, 6)],
    2: [("b", 0, 4), ("b", 1, 5), ("b", 2, 6), ("a", 0, 7), ("a", 1, 4), ("a", 2, 5), ("g", 0, 6), ("g", 1, 7),
        ("g", 2, 4), ("h", 0, 5)],
}
NU = {it: len(u) for it, u in UNITS.items()}
U0 = {1: 0, 2: NU[1] * NSEQ}


def need(eng, sem, value):
    if not isinstance(value, int) or value > 0:
        eng.wait_ge(sem, value)


def settle(eng, S):
    eng.wait_ge(S["x_in0"], 16)


def pairs(eng, body):
    body(0)
    with eng.Fori(1, NSEQ // 2) as pair:
        body(pair * 2)


def pairs_ends(eng, body):
    body(0)
    with eng.Fori(1, NSEQ // 2 - 1) as pair:
        body(pair * 2)
    body(NSEQ - 2)


def build(nc, x, early, late, out, dbg=None, upto=99):
    with ExitStack() as ctx:
        S = {n: ctx.enter_context(nc.semaphore(n)) for n in SEMAPHORES}

        def sb(name, shape, dt=F32):
            return ctx.enter_context(nc.sbuf_tensor(name, shape, dt))

        PS = ctx.enter_context(nc.psum_tensor("PS", [P, 8, 512], F32))
        X = sb("X", [P, NT, P])
        MV = sb("MV", [P, 2, NT, 2])
        RS = sb("RS", [P, 2, NT])
        SD = sb("SD", [P, NT])
        small = sb("small", [P, 512])
        WL = sb("WL", [P, LATE_N])
        KEEP_N, TEMP_N = 20480, 22200
        KEEP = sb("KEEP", [P, KEEP_N])
        TEMP = sb("TEMP", [P, TEMP_N])

        def cut(region, at):
            pos = [at]

            def take(*shape):
                n = int(np.prod(shape))
                ap = region[:, pos[0]:pos[0] + n]
                pos[0] += n
                assert pos[0] <= region.shape[1], (pos[0], region.shape)
                if len(shape) == 2:
                    ap = ap.rearrange("p (a b) -> p a b", a=shape[0])
                elif len(shape) == 3:
                    ap = ap.rearrange("p (a b c) -> p a b c", a=shape[0], b=shape[1])
                return ap
            return take

        WE = TEMP[:, 0:EARLY_N]

        def we(name):
            a, z = EARLY_AT[name]
            return WE[:, a:z]

        def wl(name):
            a, z = LATE_AT[name]
            return WL[:, a:z]

        ident = we("ident")
        sm = cut(small, 0)
        stat = sm(2, TILES, 6)
        mvt = sm(2, TILES, 2)
        ssq = sm(NT, 2)
        rnorm = sm(NT, 2)
        recip = sm(2, TILES)
        om_r, om_k = sm(1), sm(1)
        v1 = sm(NT)
        rs2 = sm(NT)
        nmr = sm(NT)
        hb2h = sm(1)

        def tiles(ap, t):
            return ap[:, bass.ds(t * TILES, TILES)]

        def bc(ap, n=P):
            return ap.unsqueeze(2).to_broadcast([P, ap.shape[1], n])

        def rows(ap, n=TILES):
            return ap.unsqueeze(1).to_broadcast([P, n, ap.shape[1]])

        ka = cut(KEEP, 0)
        QKV = ka(NT, 3, 132)
        xn, xT = ka(2, TILES, P), ka(2, SEQ)
        xc = ka(2, TILES, P)
        ta = cut(TEMP, EARLY_N)
        qn, kn = ta(2, TILES, P), ta(2, TILES, P)
        qT, kT = ta(2, SEQ), ta(2, SEQ)
        E = ta(2, 4 * SEQ)
        on, oT = ta(2, TILES, P), ta(2, SEQ)
        h1 = ta(2, SEQ)
        h2 = ta(2, HC * SEQ)
        junk = ka(4, P)
        kb = cut(KEEP, 0)
        b_xn, b_xc, b_tr, b_tk = kb(2, TILES, P), kb(2, TILES, P), kb(2, SEQ), kb(2, SEQ)
        b_xT = kb(2, SEQ + 4)
        b_xr, b_xk, b_rs, b_kr, b_ka, b_ot = [kb(2, SEQ) for _ in range(6)]
        kc = cut(KEEP, 0)
        XP = kc(NT, P)
        c_hn, c_hT, c_qT, c_y, c_yT = kc(2, TILES, P), kc(2, SEQ), kc(2, SEQ), kc(2, TILES, P), kc(2, SEQ)
        tok = kc(2, TILES, 384)
        kv = kc(2, 1024)
        tc = cut(TEMP, EARLY_N)
        qm = tc(2, 1024)
        Mbd = tc(2, 3, P)
        kd = cut(KEEP, NT * P)
        d_xc, d_xn, d_hT = kd(2, TILES, P), kd(2, TILES, P), kd(2, SEQ)
        d_G = kd(2, HC * SEQ)

        ke = cut(KEEP, 0)
        XI, VS = ke(NSEQ * SEQ), ke(NSEQ * SEQ)
        CW = ke(2, NSEQ * SEQ)
        OH = ke(2, NSEQ * SEQ // 2).bitcast(BF16)
        te = cut(TEMP, 0)
        esel, eyeb = te(256).bitcast(BF16), te(64).bitcast(BF16)
        bias2 = te(2, 192).bitcast(BF16)
        swc, hosw, nhosw = te(1), te(1), te(1)
        fbiw = te(P)
        tf = cut(TEMP, 1024)
        e_xc, e_xn = tf(2, TILES, P), tf(2, TILES, P)
        e_rh = tf(2, SEQ)
        lg, m8, ixf = tf(2, TILES, 8), tf(2, TILES, 8), tf(2, TILES, 8)
        ix = tf(2, TILES * 8).bitcast(U32)
        dd, th = tf(2, TILES), tf(2, TILES)
        cw = tf(2, 2 * TILES)
        wide = tf(2, 2 * TILES, P)
        oht = tf(2, 2 * TILES * 48).bitcast(BF16)
        r1, r2 = tf(768), tf(768)
        p0, p1, p2 = tf(384).bitcast(BF16), tf(384).bitcast(BF16), tf(384).bitcast(BF16)
        tg_ = cut(TEMP, 1024)
        hs = tg_(2, SEQ)
        hE = tg_(HC, SEQ)
        hM = tg_(2, 2, HC * SEQ)
        az, rz, ta_, tgt = tg_(3, SEQ), tg_(3, SEQ), tg_(3, SEQ), tg_(3, SEQ)
        xm, hlt = tg_(SEQ), tg_(SEQ)
        vsum, dsum = tg_(SEQ), tg_(SEQ)
        th_ = cut(TEMP, 1024)
        rf = th_(2, 2 * SEQ)
        ot = th_(2, SEQ)

        def seq(ap, t):
            return ap[:, bass.ds(t * SEQ, SEQ)]

        ones_col = QKV[:, :, 2, 128:129]
        x_in = x.rearrange("(n j p) d -> n p j d", j=TILES, p=P)
        x_out = out.rearrange("(n j p) d -> n p j d", j=TILES, p=P)
        block = ctx.enter_context(nc.Block())

        @block.sync
        def _(sp):
            for t in range(NSEQ):
                sp.dma_start(X[:, t * TILES:(t + 1) * TILES, :], x_in[t]).then_inc(S[f"x_in{t}"], 16)
            sp.dma_start(WE, early).then_inc(S["w_early"], 16)
            sp.dma_start(WL[:, :], late).then_inc(S["w_late"], 16)
            for t in range(NSEQ):
                sp.wait_ge(S["e_x"], t + 1)
                sp.dma_start(x_out[t], X[:, t * TILES:(t + 1) * TILES, :]).then_inc(S["out_done"], 16)
            sp.wait_ge(S["out_done"], 16 * NSEQ)

        @block.gpsimd
        def _(pool):
            def normed(t, k, src, n, cen, dst, sc, sn):
                pool.tensor_tensor(cen[:, k], tiles(src, t), bc(tiles(MV[:, n, :, 0], t)), ALU.subtract).then_inc(sc, 1)
                pool.wait_ge(sc, t + 1)
                pool.tensor_tensor(dst[:, k], cen[:, k], bc(tiles(RS[:, n, :], t)), ALU.mult).then_inc(sn, 1)

            pool.wait_ge(S["ln_rs"], 1)

            def a1(b):
                for k in (0, 1):
                    need(pool, S["a1_tr"], b + k - 1)
                    normed(b + k, k, X, 0, xc, xn, S["a1_xc"], S["a1_xn"])
            pairs(pool, a1)

            pool.wait_ge(S["a1_rn"], 1)

            def a2(b):
                for k in (0, 1):
                    t = b + k
                    need(pool, S["a2_tk"], t - 1)
                    pool.tensor_tensor(qn[:, k], tiles(QKV[:, :, 0, 0:P], t), bc(tiles(rnorm[:, :, 0], t)), ALU.mult)\
                        .then_inc(S["a2_qk"], 1)
                    pool.tensor_tensor(kn[:, k], tiles(QKV[:, :, 1, 0:P], t), bc(tiles(rnorm[:, :, 1], t)), ALU.mult)\
                        .then_inc(S["a2_qk"], 1)
                    pool.tensor_tensor(tiles(X, t), tiles(X, t), rows(we("b3")), ALU.add).then_inc(S["a2_xb"], 1)
            pairs(pool, a2)

            pool.wait_ge(S["ln_rs"], 2)

            def b_(b):
                for k in (0, 1):
                    need(pool, S["b_tr"], b + k - 1)
                    normed(b + k, k, X, 1, b_xc, b_xn, S["b_xc"], S["b_xn"])
                for k in (0, 1):
                    t = b + k
                    pool.wait_ge(S["b_kr"], t + 1)
                    need(pool, S["b_o"], t - 1)
                    pool.tensor_tensor(b_ka[:, k], b_kr[:, k], b_kr[:, k], ALU.mult).then_inc(S["b_ka"], 1)
            pairs(pool, b_)

            pool.wait_ge(S["ln_rs"], 3)

            def hn(t, k):
                pool.wait_ge(S["c1_x1"], 4 * t + 4)
                need(pool, S["c1_tr"], t - 1)
                pool.tensor_tensor(c_hn[:, k], tiles(XP, t), bc(tiles(rs2, t)), ALU.mult).then_inc(S["c1_hn"], 1)

            def kvs(t, k):
                for c in range(TILES):
                    pool.wait_ge(S["c1_tok"], 4 * t + c + 1)
                    need(pool, S["c1_in"], 4 * t + c - 1)
                    o = kv[:, c % 2].rearrange("p (h v k) -> p h v k", h=HEADS, v=HD)
                    kk = tok[:, k, c, P:2 * P].rearrange("p (h o k) -> p h o k", h=HEADS, o=1).to_broadcast([P, HEADS, HD, HD])
                    vv = tok[:, k, c, 2 * P:3 * P].rearrange("p (h v o) -> p h v o", h=HEADS, o=1).to_broadcast([P, HEADS, HD, HD])
                    pool.tensor_tensor(o, kk, vv, ALU.mult).then_inc(S["c1_kv"], 1)

            hn(0, 0)
            hn(1, 1)

            def c1(b):
                for k in (0, 1):
                    kvs(b + k, k)
                    if not isinstance(b, int) or b + k + 2 < NSEQ:
                        hn(b + k + 2, k)
            pairs_ends(pool, c1)

            pool.wait_ge(S["ln_rs"], 4)

            def c3(b):
                for k in (0, 1):
                    t = b + k
                    need(pool, S["c3_tr"], t - 1)
                    normed(t, k, XP, 1, d_xc, d_xn, S["c3_xc"], S["c3_xn"])
                    pool.tensor_tensor(tiles(X, t), tiles(X, t), tiles(XP, t), ALU.add).then_inc(S["c3_xa"], 1)
                    settle(pool, S)
                    pool.wait_ge(S["c3_xa"], t + 1)
                    pool.tensor_tensor(tiles(X, t), tiles(X, t), rows(we("cb2row")), ALU.add).then_inc(S["c3_xb"], 1)
            pairs(pool, c3)

            pool.wait_ge(S["ln_rs"], 5)
            pool.wait_ge(S["k_iw"], 1)

            def d0(b):
                for k in (0, 1):
                    t = b + k
                    need(pool, S["d0_tr"], t - 1)
                    normed(t, k, X, 0, e_xc, e_xn, S["d0_xc"], S["d0_xn"])
                    settle(pool, S)
                    pool.wait_ge(S["d0_xn"], t + 1)
                    pool.tensor_tensor(tiles(X, t), tiles(X, t), e_xn[:, k], ALU.add).then_inc(S["d0_xa"], 1)
                    settle(pool, S)
                    pool.wait_ge(S["d0_xa"], t + 1)
                    pool.tensor_tensor(tiles(X, t), tiles(X, t), rows(fbiw), ALU.add).then_inc(S["d0_xb"], 1)
            pairs(pool, d0)

            def iterate(it):
                z = NSEQ * (it - 1)
                s = lambda n: S[f"d_{n}"]

                def body(b):
                    for k in (0, 1):
                        t = b + k
                        pool.wait_ge(s("ln"), (t + z) + 1)
                        pool.tensor_tensor(rz, az, rz, ALU.add).then_inc(s("sp"), 1)
                        pool.wait_ge(s("U"), 2 * (t + z) + 2)
                        pool.tensor_tensor(vsum, rz[:, 0], rz[:, 1], ALU.add).then_inc(s("Va"), 1)
                        pool.wait_ge(s("Va"), (t + z) + 1)
                        pool.tensor_tensor(vsum, vsum, rz[:, 2], ALU.add).then_inc(s("Vs"), 1)
                pairs(pool, body)
            iterate(1)
            iterate(2)

        @block.vector
        def _(dve):
            def all_stats(t, k, src, n, done):
                read, done_tiles = S[f"st_a{done // NSEQ}"], S[f"st_b{done // NSEQ}"]
                for j in range(TILES):
                    last = dve.bn_stats(stat[:, k, j], src[:, bass.ds(t * TILES + j, 1), :].rearrange("p a d -> p (a d)"))
                last.then_inc(read, 1)
                settle(dve, S)
                dve.wait_ge(read, t + 1)
                for j in range(TILES):
                    last = dve.bn_aggr(mvt[:, k, j], stat[:, k, j])
                last.then_inc(done_tiles, 1)
                dve.wait_ge(done_tiles, t + 1)
                dve.tensor_copy(tiles(MV[:, n], t), mvt[:, k]).then_inc(S["st_c"], 1)

            def finish_ln(n, count, done):
                dve.wait_ge(S["st_c"], done)
                dve.tensor_scalar(v1, MV[:, n, :, 1], LN_EPS, None, ALU.add).then_inc(S["ln_var"], 1)
                dve.wait_ge(S["ln_sd"], count)
                dve.reciprocal(RS[:, n, :], SD[:, :]).then_inc(S["ln_rs" if count != 3 else "b_om"], 1)

            dve.memset(ones_col, 1.0)
            for t in range(NSEQ):
                dve.wait_ge(S[f"x_in{t}"], 16)
                all_stats(t, t % 2, X, 0, 0)
            finish_ln(0, 1, NSEQ)

            dve.wait_ge(S["w_early"], 16)

            def a1(b):
                for k in (0, 1):
                    for j in range(TILES):
                        n = 4 * (b + k) + j
                        dve.wait_ge(S["a1_mm"], n + 1)
                        dve.tensor_tensor(QKV[:, bass.ds(n, 1), :, 0:P].rearrange("p a c d -> p (a c) d"),
                                          PS[:, 2 + j, 0:384].rearrange("p (c d) -> p c d", c=3),
                                          we("bqkv").rearrange("p (c d) -> p c d", c=3), ALU.add).then_inc(S["a1_ev"], 1)
            pairs(dve, a1)
            dve.wait_ge(S["a1_nrm"], 1)
            dve.tensor_scalar(rnorm, ssq, NORM_EPS, None, ALU.max).then_inc(S["a1_max"], 1)
            dve.wait_ge(S["a1_max"], 1)
            dve.reciprocal(rnorm, rnorm).then_inc(S["a1_rn"], 1)

            def a2(b):
                O = PS[:, 6:8, 0:258].rearrange("p a (c d) -> p a c d", c=2)
                for k in (0, 1):
                    t = b + k
                    dve.wait_ge(S["a2_o"], t + 1)
                    dve.reciprocal(recip[:, k].rearrange("p (a c) -> p a c", a=2).unsqueeze(3), O[:, :, :, 128:129]).then_inc(S["a2_rc"], 1)
                    dve.wait_ge(S["a2_rc"], t + 1)
                    need(dve, S["a2_to"], t - 1)
                    dve.tensor_tensor(on[:, k].rearrange("p (a c) d -> p a c d", a=2), O[:, :, :, 0:P],
                                      recip[:, k].rearrange("p (a c) -> p a c", a=2).unsqueeze(3).to_broadcast([P, 2, 2, P]),
                                      ALU.mult).then_inc(S["a2_on"], 1)
                for k in (0, 1):
                    t = b + k
                    dve.wait_ge(S["a2_w1"], t + 1)
                    need(dve, S["a2_w2"], 4 * (t - 1))
                    dve.tensor_scalar(h1[:, k], PS[:, 1, :], we("b1"), 0.0, ALU.add, ALU.max).then_inc(S["a2_h1"], 1)
                for k in (0, 1):
                    t = b + k
                    dve.wait_ge(S["a2_w3"], t + 1)
                    dve.wait_ge(S["a2_xb"], t + 1)
                    dve.tensor_tensor(tiles(X, t), PS[:, 0, :].rearrange("p (j d) -> p j d", j=TILES), tiles(X, t),
                                      ALU.add).then_inc(S["a2_x"], 1)
                    settle(dve, S)
                    dve.wait_ge(S["a2_x"], t + 1)
                    all_stats(t, k, X, 1, NSEQ)
            pairs(dve, a2)
            dve.memset(b_xT[:, :, 0:1], 0.0)
            dve.tensor_scalar(om_r, we("mu_r"), -1.0, 1.0, ALU.mult, ALU.add)
            dve.tensor_scalar(om_k, we("mu_k"), -1.0, 1.0, ALU.mult, ALU.add)
            finish_ln(1, 2, 2 * NSEQ)

            def b_(b):
                for k in (0, 1):
                    t = b + k
                    dve.wait_ge(S["b_tk"], t + 1)
                    need(dve, S["b_r"], t - 1)
                    dve.scalar_tensor_tensor(b_xr[:, k], b_xT[:, k, 1:SEQ + 1], we("mu_r"), b_tr[:, k], ALU.mult, ALU.add)\
                        .then_inc(S["b_xr"], 1)
                    need(dve, S["b_k"], t - 1)
                    dve.scalar_tensor_tensor(b_xk[:, k], b_xT[:, k, 1:SEQ + 1], we("mu_k"), b_tk[:, k], ALU.mult, ALU.add)\
                        .then_inc(S["b_xk"], 1)
                for k in (0, 1):
                    t = b + k
                    dve.wait_ge(S["b_o"], t + 1)
                    dve.wait_ge(S["b_rs"], t + 1)
                    need(dve, S["b_x"], t - 1)
                    dve.tensor_tensor(b_ot[:, k], PS[:, 6 + k, :], b_rs[:, k], ALU.mult).then_inc(S["b_ot"], 1)
                    dve.wait_ge(S["b_ot"], t + 1)
                    dve.tensor_tensor(tiles(X, t), b_ot[:, k].rearrange("p (j d) -> p j d", j=TILES), tiles(X, t),
                                      ALU.add).then_inc(S["b_x"], 1)
                    settle(dve, S)
                    dve.wait_ge(S["b_x"], t + 1)
                    all_stats(t, k, X, 0, 2 * NSEQ)
            pairs(dve, b_)

            finish_ln(0, 3, 3 * NSEQ)
            dve.wait_ge(S["b_om"], 1)
            dve.tensor_tensor(v1, MV[:, 0, :, 1], RS[:, 0, :], ALU.mult).then_inc(S["b_om"], 1)
            dve.wait_ge(S["b_om"], 2)
            dve.tensor_tensor(v1, v1, RS[:, 0, :], ALU.mult).then_inc(S["b_om"], 1)
            dve.wait_ge(S["b_om"], 3)
            dve.tensor_scalar(v1, v1, LN_EPS, None, ALU.add).then_inc(S["ln_var"], 1)
            dve.wait_ge(S["ln_sd"], 4)
            dve.reciprocal(rs2, SD[:, :]).then_inc(S["b_om"], 1)
            dve.scalar_tensor_tensor(nmr, MV[:, 0, :, 0], -1.0, RS[:, 0, :], ALU.mult, ALU.mult).then_inc(S["b_om"], 1)
            dve.wait_ge(S["b_om"], 5)
            dve.memset(stat[:, 0, 0, 0:1], 0.0).then_inc(S["ln_rs"], 1)

            def mask_m(t, k):
                dve.wait_ge(S["c1_m"], t + 1)
                need(dve, S["c1_yin"], t - 1)
                dve.tensor_tensor(Mbd[:, k], PS[:, 2, 0:384].rearrange("p (c d) -> p c d", c=3), rows(we("blockdiag"), 3),
                                  ALU.mult).then_inc(S["c1_M"], 1)

            def chunks(t, k):
                need(dve, S["c1_ty"], t - 1)
                for c in range(TILES):
                    dve.wait_ge(S["c1_in"], 4 * t + c + 1)
                    need(dve, S["c1_red"], 4 * t + c - 1)
                    acc = PS[:, 4 + 2 * (c % 2):6 + 2 * (c % 2), :].rearrange("p a (h v k) -> p (a h) v k", h=HEADS // 2, v=HD)
                    q = tok[:, k, c, 0:P].rearrange("p (h o k) -> p h o k", h=HEADS, o=1).to_broadcast([P, HEADS, HD, HD])
                    dve.tensor_tensor(qm[:, c % 2].rearrange("p (h v k) -> p h v k", h=HEADS, v=HD), acc, q, ALU.mult)\
                        .then_inc(S["c1_qm"], 1)
                    dve.wait_ge(S["c1_qm"], 4 * t + c + 1)
                    dve.tensor_reduce(c_y[:, k, c], qm[:, c % 2].rearrange("p (h k) -> p h k", k=HD), AXX, ALU.add)\
                        .then_inc(S["c1_red"], 1)
                dve.wait_ge(S["c1_yin"], t + 1)
                dve.wait_ge(S["c1_red"], 4 * t + 4)
                dve.tensor_tensor(c_y[:, k, 1:TILES], PS[:, 3, 0:384].rearrange("p (c d) -> p c d", c=3), c_y[:, k, 1:TILES],
                                  ALU.add).then_inc(S["c1_y"], 1)

            def residual(t, k):
                dve.wait_ge(S["c1_wo"], t + 1)
                dve.tensor_tensor(tiles(XP, t), PS[:, 2, :].rearrange("p (j d) -> p j d", j=TILES), tiles(XP, t),
                                  ALU.add).then_inc(S["c1_xp"], 1)
                settle(dve, S)
                dve.wait_ge(S["c1_xp"], t + 1)
                all_stats(t, k, XP, 1, 3 * NSEQ)

            mask_m(0, 0)

            def c1(b):
                for k in (0, 1):
                    t = b + k
                    if not isinstance(t, int) or t + 1 < NSEQ:
                        mask_m(t + 1, 1 - k)
                    chunks(t, k)
                    if not isinstance(t, int) or t > 0:
                        residual(t - 1, 1 - k)
            pairs_ends(dve, c1)
            residual(NSEQ - 1, 1)
            dve.wait_ge(S["st_c"], 4 * NSEQ)
            dve.tensor_scalar(v1, MV[:, 1, :, 1], LN_EPS, None, ALU.add).then_inc(S["ln_var"], 1)
            dve.wait_ge(S["ln_sd"], 5)
            dve.reciprocal(RS[:, 1, :], SD[:, :]).then_inc(S["ln_rs"], 1)

            def c3(b):
                for lev in range(LEVELS):
                    for k in (0, 1):
                        t = b + k
                        dve.wait_ge(S["c3_w2"], 3 * b + 2 * lev + k + 1)
                        if lev < LEVELS - 1:
                            dve.tensor_scalar(d_hT[:, k], PS[:, 6 + k, :], we("cb2")[:, lev:lev + 1], None, ALU.add)\
                                .then_inc(S["c3_w2e"], 1)
                        else:
                            dve.wait_ge(S["c3_xb"], t + 1)
                            dve.tensor_tensor(tiles(X, t), PS[:, 6 + k, :].rearrange("p (j d) -> p j d", j=TILES),
                                              tiles(X, t), ALU.add).then_inc(S["c3_w2e"], 1)
                            settle(dve, S)
                            dve.wait_ge(S["c3_w2e"], 3 * b + 2 * lev + k + 1)
                            all_stats(t, k, X, 0, 4 * NSEQ)
            pairs(dve, c3)
            dve.wait_ge(S["st_c"], 5 * NSEQ)
            dve.tensor_scalar(v1, MV[:, 0, :, 1], LN_EPS, None, ALU.add).then_inc(S["ln_var"], 1)
            dve.wait_ge(S["ln_sd"], 6)
            dve.reciprocal(RS[:, 0, :], SD[:, :]).then_inc(S["ln_rs"], 1)

            dve.wait_ge(S["w_late"], 16)
            dve.tensor_copy(esel, wl("esel"))
            dve.tensor_copy(eyeb, wl("lident"))
            dve.memset(oht, 0.0)
            dve.tensor_tensor(fbiw, wl("fb2row"), wl("iwrow"), ALU.mult).then_inc(S["k_iw"], 1)
            both = WL[0:96, LATE_AT["eb2"][0]:LATE_AT["sb2"][1]]
            dve.tensor_copy(p0[0:96], both).then_inc(S["k_dve"], 1)
            dve.wait_ge(S["k_dve"], 1)
            dve.tensor_tensor(r1[0:96], both, p0[0:96], ALU.subtract).then_inc(S["k_dve"], 1)
            dve.wait_ge(S["k_dve"], 2)
            dve.tensor_copy(p1[0:96], r1[0:96]).then_inc(S["k_dve"], 1)
            dve.wait_ge(S["k_dve"], 3)
            dve.tensor_tensor(r2[0:96], r1[0:96], p1[0:96], ALU.subtract).then_inc(S["k_dve"], 1)
            dve.wait_ge(S["k_dve"], 4)
            flat = bias2.rearrange("p a b -> p (a b)")
            dve.tensor_copy(flat[0:32], p0[0:32])
            dve.tensor_copy(flat[32:64], p1[32:64])
            dve.tensor_copy(flat[64:96], r2[64:96])
            dve.wait_ge(S["k_sw"], 1)
            dve.tensor_scalar(hosw, swc, -0.25, 0.25, ALU.mult, ALU.add)
            dve.tensor_scalar(nhosw, swc, 0.25, -0.25, ALU.mult, ALU.add).then_inc(S["k_dve"], 1)
            dve.wait_ge(S["k_dve"], 5)
            dve.tensor_scalar(swc, swc, 0.5, 0.5, ALU.mult, ALU.add).then_inc(S["k_sets"], 1)
            dve.wait_ge(S["k_sets"], 1)

            def d0(b):
                for k in (0, 1):
                    t = b + k
                    dve.wait_ge(S["d0_l"], t + 1)
                    dve.tensor_tensor(lg[:, k], PS[:, 3, 0:32].rearrange("p (j e) -> p j e", j=TILES), rows(wl("rb2")), ALU.add)\
                        .then_inc(S["d0_lg"], 1)
                    settle(dve, S)
                    dve.wait_ge(S["d0_lg"], t + 1)
                    for j in range(TILES):
                        last = dve.max(m8[:, k, j], lg[:, k, j])
                    last.then_inc(S["d0_mx"], 1)
                    settle(dve, S)
                    dve.wait_ge(S["d0_mx"], t + 1)
                    for j in range(TILES):
                        last = dve.max_index(ix[:, k, 8 * j:8 * j + 8], m8[:, k, j], lg[:, k, j])
                    last.then_inc(S["d0_ix"], 1)
                    dve.tensor_tensor(dd[:, k], m8[:, k, :, 0], m8[:, k, :, 1], ALU.subtract).then_inc(S["d0_d"], 1)
                    dve.wait_ge(S["d0_ix"], t + 1)
                    dve.tensor_copy(ixf[:, k], ix[:, k].rearrange("p (j e) -> p j e", j=TILES)).then_inc(S["d0_if"], 1)
                    dve.wait_ge(S["d0_if"], t + 1)
                    need(dve, S["d0_ot"], t - 1)
                    for e in (0, 1):
                        o = oht[:, k].rearrange("p (e j g r) -> p e j g r", e=2, j=TILES, g=3)[:, e, :, :, 0:EXPERTS]
                        io = wl("iota").unsqueeze(1).unsqueeze(1).to_broadcast([P, TILES, 3, EXPERTS])
                        ie = ixf[:, k, :, e:e + 1].unsqueeze(2).to_broadcast([P, TILES, 3, EXPERTS])
                        last = dve.tensor_tensor(o, io, ie, ALU.is_equal)
                    last.then_inc(S["d0_oh"], 1)
                for k in (0, 1):
                    t = b + k
                    dve.wait_ge(S["d0_th"], t + 1)
                    dve.tensor_scalar(cw[:, k, 0:TILES], th[:, k], 1.0, hosw, ALU.add, ALU.mult)
                    dve.tensor_scalar(cw[:, k, TILES:], th[:, k], -1.0, nhosw, ALU.add, ALU.mult).then_inc(S["d0_cw"], 1)
                    dve.wait_ge(S["d0_cw"], t + 1)
                    need(dve, S["d0_ct"], t - 1)
                    dve.tensor_copy(wide[:, k], bc(cw[:, k])).then_inc(S["d0_wide"], 1)
                    dve.wait_ge(S["d0_ot"], t + 1)
                    for e in (0, 1):
                        last = dve.tensor_copy(OH[0:96, e, bass.ds(t * SEQ, SEQ)], PS[0:96, 4 + e, 0:256].bitcast(BF16))
                    last.then_inc(S["d0_ohT"], 1)
            pairs(dve, d0)

            def iterate(it):
                z = NSEQ * (it - 1)
                s = lambda n: S[f"d_{n}"]

                def masks(t, k):
                    need(dve, s("u"), U0[it] + NU[it] * (t - 1))
                    for c in range(HC):
                        dve.wait_ge(s("m"), 4 * (t + z) + c + 1)
                        dve.wait_ge(s("ge"), 5 * (t + z) + c + 2)
                        for e in (0, 1):
                            dve.tensor_tensor(hM[:, k, e, SEQ * c:SEQ * (c + 1)], hE[:, c], PS[:, 2 + e, :], ALU.mult)\
                                .then_inc(s("hm"), 1)

                def step(t):
                    dve.tensor_scalar(xm, seq(XI, t), wl("mu"), None, ALU.subtract).then_inc(s("xm"), 1)
                    dve.wait_ge(s("xm"), (t + z) + 1)
                    three = lambda ap: ap.unsqueeze(1).to_broadcast([P, 3, SEQ])
                    dve.wait_ge(s("sp"), (t + z) + 1)
                    dve.tensor_tensor(rz, rz, three(xm), ALU.mult).then_inc(s("t1"), 1)
                    dve.wait_ge(s("t1"), (t + z) + 1)
                    if it == 2:
                        dve.wait_ge(s("ev"), U0[it] + NU[it] * t + NU[it])
                        dve.scalar_tensor_tensor(ta_, ta_, 1.0, three(seq(VS, t)), ALU.add, ALU.mult).then_inc(s("t2"), 1)
                        dve.wait_ge(s("t2"), t + 1)
                        dve.scalar_tensor_tensor(rz, ta_, 0.5, rz, ALU.mult, ALU.subtract).then_inc(s("vn"), 1)
                        dve.wait_ge(s("vn"), t + 1)
                    dve.tensor_scalar(rz[:, 0], rz[:, 0], swc, None, ALU.mult).then_inc(s("U"), 1)
                    dve.tensor_tensor(rz[:, 1:3], rz[:, 1:3], CW[:, :, bass.ds(t * SEQ, SEQ)], ALU.mult).then_inc(s("U"), 1)
                    dve.wait_ge(s("U"), 2 * (t + z) + 2)
                    dve.wait_ge(s("ev"), U0[it] + NU[it] * t + NU[it])
                    dve.scalar_tensor_tensor(tgt, tgt, 1.0, rz, ALU.add, ALU.mult).then_inc(s("gU"), 1)
                    dve.wait_ge(s("gU"), (t + z) + 1)
                    dve.tensor_tensor(dsum, tgt[:, 0], tgt[:, 1], ALU.add).then_inc(s("Da"), 1)
                    dve.wait_ge(s("Da"), (t + z) + 1)
                    dve.tensor_tensor(dsum, dsum, tgt[:, 2], ALU.add).then_inc(s("Ds"), 1)
                    dve.wait_ge(s("Ds"), (t + z) + 1)
                    sign = -1.0 if it == 1 else 1.0
                    dve.scalar_tensor_tensor(dsum, hlt, 1.0, dsum, ALU.add, ALU.mult).then_inc(s("hx"), 1)
                    dve.wait_ge(s("Vs"), (t + z) + 1)
                    if it == 2:
                        dve.tensor_tensor(vsum, vsum, seq(VS, t), ALU.subtract).then_inc(s("v2"), 1)
                        dve.wait_ge(s("v2"), t + 1)
                    dve.scalar_tensor_tensor(vsum, hlt, 1.0, vsum, ALU.add, ALU.mult).then_inc(s("hv"), 1)
                    dve.wait_ge(s("hx"), (t + z) + 1)
                    dve.scalar_tensor_tensor(seq(XI, t), dsum, sign * 0.1 * 0.5 * 0.5, seq(XI, t), ALU.mult, ALU.add)\
                        .then_inc(s("x"), 1)
                    dve.wait_ge(s("hv"), (t + z) + 1)
                    if it == 2:
                        dve.scalar_tensor_tensor(seq(VS, t), vsum, 0.5, seq(VS, t), ALU.mult, ALU.add).then_inc(s("v"), 1)
                        dve.wait_ge(s("v"), NSEQ + t + 1)
                    else:
                        dve.tensor_scalar(seq(VS, t), vsum, -0.5, None, ALU.mult).then_inc(s("v"), 1)
                        dve.wait_ge(s("v"), t + 1)
                    dve.wait_ge(s("x"), (t + z) + 1)

                masks(0, 0)

                def body(b):
                    for k in (0, 1):
                        t = b + k
                        if not isinstance(t, int) or t + 1 < NSEQ:
                            masks(t + 1, 1 - k)
                        step(t)
                pairs_ends(dve, body)
            iterate(1)
            iterate(2)

            def refine(b):
                for k in (0, 1):
                    t = b + k
                    dve.wait_ge(S["e_2"], t + 1)
                    need(dve, S["e_x"], t - 1)
                    dve.tensor_tensor(ot[:, k].rearrange("p (j d) -> p j d", j=TILES),
                                      PS[:, 2 + k, :].rearrange("p (j d) -> p j d", j=TILES), rows(wl("iwrow")), ALU.mult)\
                        .then_inc(S["e_t"], 1)
                    dve.wait_ge(S["e_t"], t + 1)
                    dve.tensor_tensor(tiles(X, t), tiles(X, t), ot[:, k].rearrange("p (j d) -> p j d", j=TILES), ALU.add)\
                        .then_inc(S["e_x"], 1)
            pairs(dve, refine)

        @block.scalar
        def _(act):
            def root(count):
                act.wait_ge(S["ln_var"], count)
                act.activation(SD[:, :], v1, ACT.Sqrt).then_inc(S["ln_sd"], 1)

            root(1)
            act.wait_ge(S["w_early"], 16)

            def a1(b):
                for k in (0, 1):
                    t = b + k
                    act.wait_ge(S["a1_tr"], t + 1)
                    need(act, S["a1_mm"], 4 * (t - 1))
                    act.activation(xT[:, k], PS[:, k, :], ACT.Copy).then_inc(S["a1_xt"], 1)
                for k in (0, 1):
                    for j in range(TILES):
                        n = 4 * (b + k) + j
                        act.wait_ge(S["a1_ev"], n + 1)
                        for c in (0, 1):
                            need(act, S["a1_sq"], 2 * n + c - 3)
                            act.activation(junk[:, 2 * (j % 2) + c], QKV[:, bass.ds(n, 1), c, 0:P].rearrange("p a d -> p (a d)"),
                                           ACT.Square, accum_out=ssq[:, bass.ds(n, 1), c]).then_inc(S["a1_sq"], 1)
            pairs(act, a1)
            act.wait_ge(S["a1_sq"], 2 * NT)
            act.activation(ssq, ssq, ACT.Sqrt).then_inc(S["a1_nrm"], 1)

            def a2(b):
                for k in (0, 1):
                    t = b + k
                    act.wait_ge(S["a2_tq"], t + 1)
                    need(act, S["a2_s"], 4 * (t - 1))
                    act.activation(qT[:, k], PS[:, 0, :], ACT.Copy).then_inc(S["a2_qT"], 1)
                    act.wait_ge(S["a2_tk"], t + 1)
                    act.activation(kT[:, k], PS[:, 1, :], ACT.Copy).then_inc(S["a2_kT"], 1)
                    need(act, S["a2_o"], t - 1)
                    for c in range(TILES):
                        act.wait_ge(S["a2_s"], 4 * t + c + 1)
                        act.activation(E[:, k, SEQ * c:SEQ * (c + 1)], PS[:, 2 + c, :], ACT.Exp).then_inc(S["a2_E"], 1)
                for k in (0, 1):
                    t = b + k
                    act.wait_ge(S["a2_to"], t + 1)
                    need(act, S["a2_w1"], t - 1)
                    act.activation(oT[:, k], PS[:, 0, :], ACT.Copy).then_inc(S["a2_oT"], 1)
                for k in (0, 1):
                    t = b + k
                    need(act, S["a2_w3"], t - 1)
                    for c in range(HC):
                        act.wait_ge(S["a2_w2"], 4 * t + c + 1)
                        act.activation(h2[:, k, SEQ * c:SEQ * (c + 1)], PS[:, 2 + c, :], ACT.Relu,
                                       bias=we("b2")[:, c:c + 1]).then_inc(S["a2_h2"], 1)
            pairs(act, a2)
            root(2)

            act.wait_ge(S["ln_rs"], 2)

            def b_(b):
                for k in (0, 1):
                    t = b + k
                    act.wait_ge(S["b_tr"], t + 1)
                    need(act, S["b_xk"], t - 1)
                    act.activation(b_xT[:, k, 1:SEQ + 1], PS[:, k, :], ACT.Copy).then_inc(S["b_xT"], 1)
                    act.wait_ge(S["b_xT"], t + 1)
                    act.activation(b_tr[:, k], b_xT[:, k, 0:SEQ], ACT.Copy, scale=om_r)
                    act.activation(b_tk[:, k], b_xT[:, k, 0:SEQ], ACT.Copy, scale=om_k).then_inc(S["b_tk"], 1)
                for k in (0, 1):
                    t = b + k
                    act.wait_ge(S["b_r"], t + 1)
                    need(act, S["b_ot"], t - 1)
                    act.activation(b_rs[:, k], PS[:, 2 + k, :], ACT.Sigmoid).then_inc(S["b_rs"], 1)
                    act.wait_ge(S["b_k"], t + 1)
                    need(act, S["b_ka"], t - 1)
                    act.activation(b_kr[:, k], PS[:, 4 + k, :], ACT.Relu).then_inc(S["b_kr"], 1)
            pairs(act, b_)
            root(3)
            root(4)

            act.wait_ge(S["ln_rs"], 3)

            def x1(t):
                for j in range(TILES):
                    n = t * TILES + j
                    act.activation(XP[:, bass.ds(n, 1), :].rearrange("p a d -> p (a d)"),
                                   X[:, bass.ds(n, 1), :].rearrange("p a d -> p (a d)"), ACT.Identity,
                                   scale=RS[:, 0, bass.ds(n, 1)], bias=nmr[:, bass.ds(n, 1)]).then_inc(S["c1_x1"], 1)

            def project(t, k):
                act.wait_ge(S["c1_tr"], t + 1)
                need(act, S["c1_q"], t - 1)
                act.activation(c_hT[:, k], PS[:, 0, :], ACT.Identity, scale=we("ln1_g"), bias=we("ln1_b")).then_inc(S["c1_hT"], 1)
                need(act, S["c1_red"], 4 * (t - 1))
                for j in range(TILES):
                    act.wait_ge(S["c1_mm"], 4 * t + j + 1)
                    act.activation(tok[:, k, j], PS[:, (1 + j) % 2, 0:384], ACT.Copy).then_inc(S["c1_tok"], 1)
                act.wait_ge(S["c1_q"], t + 1)
                need(act, S["c1_yin"], t - 1)
                act.activation(c_qT[:, k], PS[:, 1, :], ACT.Copy).then_inc(S["c1_qT"], 1)

            def turned(t, k):
                act.wait_ge(S["c1_ty"], t + 1)
                need(act, S["c1_wo"], t - 1)
                act.activation(c_yT[:, k], PS[:, 0, :], ACT.Copy).then_inc(S["c1_yT"], 1)

            x1(0)
            x1(1)
            project(0, 0)

            def c1(b):
                for k in (0, 1):
                    t = b + k
                    if not isinstance(t, int) or t + 1 < NSEQ:
                        project(t + 1, 1 - k)
                    if not isinstance(t, int) or t > 0:
                        turned(t - 1, 1 - k)
                    if not isinstance(b, int) or t + 2 < NSEQ:
                        x1(t + 2)
            pairs_ends(act, c1)
            turned(NSEQ - 1, 1)
            root(5)

            def c3(b):
                for k in (0, 1):
                    t = b + k
                    act.wait_ge(S["c3_tr"], t + 1)
                    need(act, S["c3_w1"], 12 * b - 4 + 4 * k)
                    act.activation(d_hT[:, k], PS[:, k, :], ACT.Identity, scale=we("ln2_g"), bias=we("ln2_b"))\
                        .then_inc(S["c3_hT"], 1)
                for lev in range(LEVELS):
                    for k in (0, 1):
                        need(act, S["c3_w2"], 3 * b + 2 * lev + k - 1)
                        for c in range(HC):
                            act.wait_ge(S["c3_w1"], 12 * b + 8 * lev + 4 * k + c + 1)
                            act.activation(d_G[:, k, SEQ * c:SEQ * (c + 1)], PS[:, 2 + c, :], ACT.Gelu_apprx_tanh,
                                           bias=we("cb1")[:, 4 * lev + c:4 * lev + c + 1]).then_inc(S["c3_g"], 1)
            pairs(act, c3)
            root(6)

            act.wait_ge(S["ln_rs"], 5)
            act.wait_ge(S["w_late"], 16)
            act.activation(swc, wl("shw"), ACT.Tanh, scale=0.5).then_inc(S["k_sw"], 1)

            def d0(b):
                for k in (0, 1):
                    t = b + k
                    act.wait_ge(S["d0_tr"], t + 1)
                    act.activation(seq(XI, t), PS[:, k, :], ACT.Copy).then_inc(S["d0_xi"], 1)
                for k in (0, 1):
                    t = b + k
                    act.wait_ge(S["d0_r"], t + 1)
                    need(act, S["d0_l"], t - 1)
                    act.activation(e_rh[:, k], PS[:, 2, :], ACT.Gelu, bias=wl("rb1")).then_inc(S["d0_rh"], 1)
                for k in (0, 1):
                    t = b + k
                    act.wait_ge(S["d0_d"], t + 1)
                    need(act, S["d0_cw"], t - 1)
                    act.activation(th[:, k], dd[:, k], ACT.Tanh, scale=0.5).then_inc(S["d0_th"], 1)
                for k in (0, 1):
                    t = b + k
                    for e in (0, 1):
                        act.wait_ge(S["d0_ct"], t + 1)
                        last = act.activation(CW[:, e, bass.ds(t * SEQ, SEQ)], PS[:, 6 + e, :], ACT.Copy)
                    last.then_inc(S["d0_C"], 1)
            pairs(act, d0)

            def iterate(it):
                z = NSEQ * (it - 1)
                s = lambda n: S[f"d_{n}"]

                def hidden(t, k):
                    need(act, s("u"), U0[it] + NU[it] * (t - 1))
                    act.wait_ge(s("g"), 5 * (t + z) + 1)
                    act.activation(hs[0:96, k], PS[0:96, 0, :], ACT.Gelu, bias=wl("g1b")[0:96]).then_inc(s("ge"), 1)
                    for c in range(HC):
                        act.wait_ge(s("g"), 5 * (t + z) + c + 2)
                        need(act, s("hm"), 8 * ((t + z) - 1) + 2 * c + 2)
                        act.activation(hE[:, c], PS[:, (c + 1) % 2, :], ACT.Gelu, bias=wl("eb1")[:, c:c + 1]).then_inc(s("ge"), 1)

                def control(t):
                    for u, (part, e, bank) in enumerate(UNITS[it]):
                        act.wait_ge(s("u"), U0[it] + NU[it] * t + u + 1)
                        if part == "b":
                            if e == 0:
                                need(act, s("x"), (t + z))
                            act.activation(az[:, e], PS[:, bank, :], ACT.Abs)
                            act.activation(rz[:, e], PS[:, bank, :], ACT.Relu).then_inc(s("ev"), 1)
                            if e == 2:
                                act.wait_ge(s("ev"), U0[it] + NU[it] * t + u + 1)
                                act.activation(az, az, ACT.Exp, scale=-1.0).then_inc(s("ex"), 1)
                                act.wait_ge(s("ex"), (t + z) + 1)
                                act.activation(az, az, ACT.Ln, bias=1.0).then_inc(s("ln"), 1)
                        elif part == "h":
                            act.activation(hlt, PS[:, bank, :], ACT.Tanh, scale=0.5, bias=hb2h).then_inc(s("ev"), 1)
                        else:
                            act.activation((ta_ if part == "a" else tgt)[:, e], PS[:, bank, :], ACT.Tanh, scale=0.5)\
                                .then_inc(s("ev"), 1)

                hidden(0, 0)

                def body(b):
                    for k in (0, 1):
                        t = b + k
                        if not isinstance(t, int) or t + 1 < NSEQ:
                            hidden(t + 1, 1 - k)
                        control(t)
                pairs_ends(act, body)
            act.wait_ge(S["k_sets"], 1)
            act.activation(hb2h, wl("hb2"), ACT.Copy, scale=0.5).then_inc(S["k_sw"], 1)
            act.wait_ge(S["k_sw"], 2)
            act.wait_ge(S["d0_ohT"], NSEQ)
            act.wait_ge(S["d0_xb"], NSEQ)
            iterate(1)
            iterate(2)

            act.wait_ge(S["d_x"], 2 * NSEQ)

            def refine(b):
                for k in (0, 1):
                    t = b + k
                    need(act, S["e_2"], t - 1)
                    for c in (0, 1):
                        act.wait_ge(S["e_1"], 2 * t + c + 1)
                        act.activation(rf[:, k, SEQ * c:SEQ * (c + 1)], PS[:, c, :], ACT.Gelu, bias=wl("fb1")[:, c:c + 1])\
                            .then_inc(S["e_g"], 1)
            pairs(act, refine)

        @block.tensor
        def _(pe):
            def turn(bank, src, k, eye):
                for j in range(TILES):
                    last = pe.transpose(PS[:, bank, P * j:P * (j + 1)], src[:, k, j], eye)
                return last

            pe.wait_ge(S["w_early"], 16)

            def a1(b):
                for k in (0, 1):
                    t = b + k
                    pe.wait_ge(S["a1_xn"], t + 1)
                    need(pe, S["a1_xt"], t - 1)
                    turn(k, xn, k, ident).then_inc(S["a1_tr"], 1)
                for k in (0, 1):
                    t = b + k
                    pe.wait_ge(S["a1_xt"], t + 1)
                    for j in range(TILES):
                        need(pe, S["a1_ev"], 4 * (t - 1) + j + 1)
                        pe.matmul(PS[:, 2 + j, 0:384], xT[:, k, P * j:P * (j + 1)], we("wqkv"), start=True, stop=True)\
                            .then_inc(S["a1_mm"], 1)
            pairs(pe, a1)

            def qk_turn(t, k):
                pe.wait_ge(S["a2_qk"], 2 * t + 2)
                if k == 0:
                    need(pe, S["a2_x"], t)
                    need(pe, S["a2_h1"], t)
                else:
                    pe.wait_ge(S["a2_qT"], t)
                    pe.wait_ge(S["a2_kT"], t)
                turn(0, qn, k, ident).then_inc(S["a2_tq"], 1)
                turn(1, kn, k, ident).then_inc(S["a2_tk"], 1)

            def scores(t, k):
                pe.wait_ge(S["a2_qT"], t + 1)
                pe.wait_ge(S["a2_kT"], t + 1)
                for c in range(TILES):
                    if k == 0:
                        need(pe, S["a2_h2"], 4 * (t - 1) + c + 1)
                    else:
                        pe.wait_ge(S["a2_E"], 4 * (t - 1) + c + 1)
                    pe.matmul(PS[:, 2 + c, :], kT[:, k, P * c:P * (c + 1)], qT[:, k], start=True, stop=True)\
                        .then_inc(S["a2_s"], 1)

            def values(t, k):
                pe.wait_ge(S["a2_E"], 4 * t + 4)
                need(pe, S["a2_on"], t)
                for j in range(TILES):
                    for c in range(TILES):
                        last = pe.matmul(PS[:, 6 + j // 2, 129 * (j % 2):129 * (j % 2) + 129],
                                         E[:, k, SEQ * c + P * j:SEQ * c + P * (j + 1)],
                                         QKV[:, bass.ds(t * TILES + c, 1), 2, 0:129].rearrange("p a d -> p (a d)"),
                                         start=c == 0, stop=c == TILES - 1)
                last.then_inc(S["a2_o"], 1)

            def o_turn(t, k):
                pe.wait_ge(S["a2_on"], t + 1)
                if k == 0:
                    pe.wait_ge(S["a2_qT"], t + 2)
                else:
                    pe.wait_ge(S["a2_oT"], t)
                turn(0, on, k, ident).then_inc(S["a2_to"], 1)

            def mlp1(t, k):
                pe.wait_ge(S["a2_oT"], t + 1)
                if k == 0:
                    pe.wait_ge(S["a2_kT"], t + 2)
                else:
                    pe.wait_ge(S["a2_h1"], t)
                pe.matmul(PS[:, 1, :], we("w1"), oT[:, k], start=True, stop=True).then_inc(S["a2_w1"], 1)

            def mlp2(t, k):
                pe.wait_ge(S["a2_h1"], t + 1)
                for c in range(HC):
                    if k == 0:
                        pe.wait_ge(S["a2_E"], 4 * (t + 1) + c + 1)
                    else:
                        pe.wait_ge(S["a2_h2"], 4 * (t - 1) + c + 1)
                    pe.matmul(PS[:, 2 + c, :], we("w2")[:, P * c:P * (c + 1)], h1[:, k], start=True, stop=True)\
                        .then_inc(S["a2_w2"], 1)

            def mlp3(t, k):
                pe.wait_ge(S["a2_h2"], 4 * t + 4)
                if k == 0:
                    pe.wait_ge(S["a2_oT"], t + 2)
                else:
                    pe.wait_ge(S["a2_x"], t)
                for j in range(TILES):
                    for c in range(HC):
                        last = pe.matmul(PS[:, 0, P * j:P * (j + 1)], h2[:, k, SEQ * c + P * j:SEQ * c + P * (j + 1)],
                                         we("w3")[:, P * c:P * (c + 1)], start=c == 0, stop=c == HC - 1)
                last.then_inc(S["a2_w3"], 1)

            def a2(b):
                qk_turn(b, 0)
                scores(b, 0)
                qk_turn(b + 1, 1)
                values(b, 0)
                scores(b + 1, 1)
                o_turn(b, 0)
                values(b + 1, 1)
                mlp1(b, 0)
                o_turn(b + 1, 1)
                mlp2(b, 0)
                mlp1(b + 1, 1)
                mlp3(b, 0)
                mlp2(b + 1, 1)
                mlp3(b + 1, 1)
            pe.wait_ge(S["a1_rn"], 1)
            pairs(pe, a2)

            pe.wait_ge(S["ln_rs"], 2)

            def b_(b):
                for k in (0, 1):
                    t = b + k
                    pe.wait_ge(S["b_xn"], t + 1)
                    need(pe, S["b_xT"], t - 1)
                    turn(k, b_xn, k, ident).then_inc(S["b_tr"], 1)
                for k in (0, 1):
                    t = b + k
                    pe.wait_ge(S["b_xr"], t + 1)
                    need(pe, S["b_rs"], t - 1)
                    for j in range(TILES):
                        last = pe.matmul(PS[:, 2 + k, P * j:P * (j + 1)], b_xr[:, k, P * j:P * (j + 1)], we("wr"),
                                         start=True, stop=True)
                    last.then_inc(S["b_r"], 1)
                    pe.wait_ge(S["b_xk"], t + 1)
                    need(pe, S["b_kr"], t - 1)
                    pe.matmul(PS[:, 4 + k, :], we("wk"), b_xk[:, k], start=True, stop=True).then_inc(S["b_k"], 1)
                for k in (0, 1):
                    t = b + k
                    pe.wait_ge(S["b_ka"], t + 1)
                    need(pe, S["b_ot"], t - 1)
                    for j in range(TILES):
                        last = pe.matmul(PS[:, 6 + k, P * j:P * (j + 1)], b_ka[:, k, P * j:P * (j + 1)], we("wv"),
                                         start=True, stop=True)
                    last.then_inc(S["b_o"], 1)
            pairs(pe, b_)

            pe.wait_ge(S["ln_rs"], 3)

            def project(t, k):
                pe.wait_ge(S["c1_hn"], t + 1)
                need(pe, S["c1_tok"], 4 * t)
                need(pe, S["c1_yT"], t - 2)
                turn(0, c_hn, k, ident).then_inc(S["c1_tr"], 1)
                pe.wait_ge(S["c1_hT"], t + 1)
                need(pe, S["c1_qT"], t)
                for j in range(TILES):
                    if j >= 2:
                        pe.wait_ge(S["c1_tok"], 4 * t + j - 1)
                    pe.matmul(PS[:, (1 + j) % 2, 0:384], c_hT[:, k, P * j:P * (j + 1)], we("lqkv"), start=True, stop=True)\
                        .then_inc(S["c1_mm"], 1)
                pe.wait_ge(S["c1_tok"], 4 * t + 3)
                pe.matmul(PS[:, 1, :], we("lqkv")[:, 0:P], c_hT[:, k], start=True, stop=True).then_inc(S["c1_q"], 1)
                pe.wait_ge(S["c1_tok"], 4 * t + 4)
                need(pe, S["c1_M"], t)
                need(pe, S["c1_xp"], t - 2)
                for m in range(3):
                    for c in range(m + 1):
                        last = pe.matmul(PS[:, 2, P * m:P * (m + 1)], tok[:, k, c, P:2 * P], tok[:, k, c, 2 * P:3 * P],
                                         start=c == 0, stop=c == m)
                last.then_inc(S["c1_m"], 1)

            def attend(t, k):
                pe.wait_ge(S["c1_M"], t + 1)
                pe.wait_ge(S["c1_qT"], t + 1)
                need(pe, S["c1_y"], t)
                for c in range(1, TILES):
                    last = pe.matmul(PS[:, 3, P * (c - 1):P * c], c_qT[:, k, P * c:P * (c + 1)], Mbd[:, k, c - 1],
                                     start=True, stop=True)
                last.then_inc(S["c1_yin"], 1)
                for c in range(TILES):
                    pe.wait_ge(S["c1_kv"], 4 * t + c + 1)
                    need(pe, S["c1_qm"], 4 * t + c - 1)
                    for h in (0, 1):
                        last = pe.matmul(PS[:, 4 + 2 * (c % 2) + h, :], we("tril"), kv[:, c % 2, SEQ * h:SEQ * (h + 1)],
                                         start=True, stop=True)
                    last.then_inc(S["c1_in"], 1)

            def finish(t, k, ahead):
                pe.wait_ge(S["c1_y"], t + 1)
                pe.wait_ge(S["c1_tok"], 4 * ahead)
                turn(0, c_y, k, ident).then_inc(S["c1_ty"], 1)
                pe.wait_ge(S["c1_yT"], t + 1)
                pe.wait_ge(S["c1_M"], ahead)
                need(pe, S["c1_xp"], t)
                for j in range(TILES):
                    last = pe.matmul(PS[:, 2, P * j:P * (j + 1)], c_yT[:, k, P * j:P * (j + 1)], we("lwo"), start=True, stop=True)
                last.then_inc(S["c1_wo"], 1)

            project(0, 0)

            def c1(b):
                for k in (0, 1):
                    t = b + k
                    if not isinstance(t, int) or t + 1 < NSEQ:
                        project(t + 1, 1 - k)
                    attend(t, k)
                    if not isinstance(t, int) or t > 0:
                        finish(t - 1, 1 - k, min(t + 2, NSEQ) if isinstance(t, int) else t + 2)
            pairs_ends(pe, c1)
            finish(NSEQ - 1, 1, NSEQ)

            pe.wait_ge(S["ln_rs"], 4)

            def c3(b):
                for k in (0, 1):
                    t = b + k
                    pe.wait_ge(S["c3_xn"], t + 1)
                    need(pe, S["c3_hT"], t - 1)
                    turn(k, d_xn, k, ident).then_inc(S["c3_tr"], 1)
                for lev in range(LEVELS):
                    for k in (0, 1):
                        if lev == 0:
                            pe.wait_ge(S["c3_hT"], b + k + 1)
                        else:
                            pe.wait_ge(S["c3_w2e"], 3 * b + 2 * (lev - 1) + k + 1)
                        for c in range(HC):
                            need(pe, S["c3_g"], 12 * b + 8 * lev + 4 * k + c - 3)
                            pe.matmul(PS[:, 2 + c, :], we("cw1")[:, 512 * lev + P * c:512 * lev + P * (c + 1)], d_hT[:, k],
                                      start=True, stop=True).then_inc(S["c3_w1"], 1)
                    for k in (0, 1):
                        pe.wait_ge(S["c3_g"], 12 * b + 8 * lev + 4 * k + 4)
                        need(pe, S["c3_w2e"], 3 * b + 2 * lev + k - 1)
                        w2 = we("cw2")[:, 512 * lev:512 * (lev + 1)]
                        if lev < LEVELS - 1:
                            for c in range(HC):
                                last = pe.matmul(PS[:, 6 + k, :], w2[:, P * c:P * (c + 1)], d_G[:, k, SEQ * c:SEQ * (c + 1)],
                                                 start=c == 0, stop=c == HC - 1)
                        else:
                            for j in range(TILES):
                                for c in range(HC):
                                    last = pe.matmul(PS[:, 6 + k, P * j:P * (j + 1)],
                                                     d_G[:, k, SEQ * c + P * j:SEQ * c + P * (j + 1)],
                                                     w2[:, P * c:P * (c + 1)], start=c == 0, stop=c == HC - 1)
                        last.then_inc(S["c3_w2"], 1)
            pairs(pe, c3)

            pe.wait_ge(S["ln_rs"], 5)
            pe.wait_ge(S["w_late"], 16)
            pe.wait_ge(S["k_sets"], 1)

            def d0(b):
                for k in (0, 1):
                    t = b + k
                    pe.wait_ge(S["d0_xn"], t + 1)
                    need(pe, S["d0_xi"], t - 1)
                    turn(k, e_xn, k, wl("lident")).then_inc(S["d0_tr"], 1)
                for k in (0, 1):
                    t = b + k
                    pe.wait_ge(S["d0_xi"], t + 1)
                    need(pe, S["d0_rh"], t)
                    pe.matmul(PS[:, 2, :], wl("rw1"), seq(XI, t), start=True, stop=True).then_inc(S["d0_r"], 1)
                for k in (0, 1):
                    t = b + k
                    pe.wait_ge(S["d0_rh"], t + 1)
                    need(pe, S["d0_lg"], t)
                    for j in range(TILES):
                        last = pe.matmul(PS[:, 3, 8 * j:8 * j + 8], e_rh[:, k, P * j:P * (j + 1)], wl("rw2"), start=True, stop=True)
                    last.then_inc(S["d0_l"], 1)
                for k in (0, 1):
                    t = b + k
                    pe.wait_ge(S["d0_oh"], t + 1)
                    need(pe, S["d0_ohT"], t)
                    for e in (0, 1):
                        for j in range(TILES):
                            last = pe.transpose(PS[0:96, 4 + e, 64 * j:64 * (j + 1)].bitcast(BF16),
                                                oht[:, k, 96 * (4 * e + j):96 * (4 * e + j + 1)], eyeb)
                    last.then_inc(S["d0_ot"], 1)
                    pe.wait_ge(S["d0_wide"], t + 1)
                    need(pe, S["d0_C"], t)
                    for e in (0, 1):
                        for j in range(TILES):
                            last = pe.transpose(PS[:, 6 + e, P * j:P * (j + 1)], wide[:, k, TILES * e + j], wl("lident"))
                    last.then_inc(S["d0_ct"], 1)
            pairs(pe, d0)

            pe.wait_ge(S["d0_ohT"], NSEQ)
            pe.wait_ge(S["d0_C"], NSEQ)

            def iterate(it):
                z = NSEQ * (it - 1)
                s = lambda n: S[f"d_{n}"]

                def hidden(t):
                    for g in range(1 + HC):
                        need(pe, s("ge"), 5 * (t + z) + g - 1 if g >= 2 else 5 * (t + z))
                        m = 96 if g == 0 else P
                        bank = g % 2
                        w = [(wl("g1x"), XI), (wl("g1v"), VS)] if g == 0 else \
                            [(wl(n)[:, P * (g - 1):P * g], r) for n, r in (("ew1x", XI), ("ew1v", VS))]
                        if it == 1:
                            w = w[:1]
                        for n, (lhs, state) in enumerate(w):
                            last = pe.matmul(PS[0:m, bank, :], lhs, seq(state, t), start=n == 0, stop=n == len(w) - 1)
                        last.then_inc(s("g"), 1)

                def mask(t, c):
                    need(pe, s("hm"), 8 * (t + z) + 2 * c)
                    for e in (0, 1):
                        last = pe.matmul(PS[:, 2 + e, :], esel[0:96, P * c:P * (c + 1)], OH[0:96, e, bass.ds(t * SEQ, SEQ)],
                                         start=True, stop=True)
                    last.then_inc(s("m"), 1)

                def unit(t, k, u):
                    part, e, bank = UNITS[it][u]
                    before = [v for v in range(NU[it]) if UNITS[it][v][2] == bank and v < u]
                    later = [v for v in range(NU[it]) if UNITS[it][v][2] == bank]
                    need(pe, s("ev"), U0[it] + NU[it] * t + before[-1] + 1 if before else U0[it] + NU[it] * (t - 1) + later[-1] + 1)
                    if part == "h":
                        pe.matmul(PS[:, bank, :], wl("hw2")[0:96], hs[0:96, k], start=True, stop=True).then_inc(s("u"), 1)
                        return
                    col = P * "abg".index(part)
                    pe.matmul(PS[:, bank, :], bias2[0:96, 0 if e else 1, col:col + P],
                              OH[0:96, max(e - 1, 0), bass.ds(t * SEQ, SEQ)], start=True, stop=False)
                    if e == 0:
                        pe.matmul(PS[:, bank, :], wl("sw2")[0:96, col:col + P], hs[0:96, k], start=False, stop=True)\
                            .then_inc(s("u"), 1)
                        return
                    for c in range(HC):
                        last = pe.matmul(PS[:, bank, :], wl("ew2")[:, 384 * c + col:384 * c + col + P],
                                         hM[:, k, e - 1, SEQ * c:SEQ * (c + 1)], start=False, stop=c == HC - 1)
                    last.then_inc(s("u"), 1)

                hidden(0)
                for c in range(HC):
                    mask(0, c)

                def body(b):
                    for k in (0, 1):
                        t = b + k
                        more = not isinstance(t, int) or t + 1 < NSEQ
                        if more:
                            hidden(t + 1)
                        pe.wait_ge(s("ge"), 5 * (t + z) + 1)
                        for u in range(NU[it]):
                            if u == 1:
                                pe.wait_ge(s("hm"), 8 * (t + z) + 8)
                            unit(t, k, u)
                            if more and u < HC:
                                mask(t + 1, u)
                pairs_ends(pe, body)
            iterate(1)
            pe.wait_ge(S["d_x"], NSEQ)
            pe.wait_ge(S["d_v"], NSEQ)
            iterate(2)

            pe.wait_ge(S["d_x"], 2 * NSEQ)
            pe.wait_ge(S["d_ev"], U0[2] + NU[2] * NSEQ)

            def refine(b):
                for k in (0, 1):
                    t = b + k
                    for c in (0, 1):
                        need(pe, S["e_g"], 2 * t + c - 1)
                        pe.matmul(PS[:, c, :], wl("fw1")[:, P * c:P * (c + 1)], seq(XI, t), start=True, stop=True)\
                            .then_inc(S["e_1"], 1)
                for k in (0, 1):
                    t = b + k
                    pe.wait_ge(S["e_g"], 2 * t + 2)
                    need(pe, S["e_t"], t - 1)
                    for j in range(TILES):
                        for c in (0, 1):
                            last = pe.matmul(PS[:, 2 + k, P * j:P * (j + 1)], rf[:, k, SEQ * c + P * j:SEQ * c + P * (j + 1)],
                                             wl("fw2")[:, P * c:P * (c + 1)], start=c == 0, stop=c == 1)
                    last.then_inc(S["e_2"], 1)
            pairs(pe, refine)


def pack_early(i):
    a = np.zeros((P, EARLY_N), np.float32)

    def put(name, v):
        s, z = EARLY_AT[name]
        v = np.asarray(v).reshape(-1, z - s) if np.ndim(v) != 1 or z - s > 1 else np.asarray(v)[:, None]
        a[:v.shape[0] if v.shape[0] > 1 else P, s:z] = v

    put("ident", np.eye(P, dtype=np.float32))
    put("tril", np.triu(np.ones((P, P), np.float32)))
    put("blockdiag", np.kron(np.eye(HEADS, dtype=np.float32), np.ones((HD, HD), np.float32)))
    put("wqkv", np.concatenate([i["L0_attn_Wq"].T, i["L0_attn_Wk"].T, i["L0_attn_Wv"].T], 1))
    put("bqkv", np.concatenate([i["L0_attn_bq"], i["L0_attn_bk"], i["L0_attn_bv"]])[None])
    put("w1", i["L0_attn_W1"].T)
    put("b1", i["L0_attn_b1"])
    put("w2", i["L0_attn_W2"].T)
    put("b2", i["L0_attn_b2"].reshape(HC, P).T)
    put("w3", i["L0_attn_W3"].T.reshape(HC, P, P).transpose(1, 0, 2).reshape(P, 512))
    put("b3", i["L0_attn_b3"][None])
    put("wr", i["L0_ffn_W_r"].T)
    put("wk", i["L0_ffn_W_k"].T)
    put("wv", i["L0_ffn_W_v"].T)
    for n in ("mu_r", "mu_k"):
        put(n, i["L0_ffn_" + n])
    for n in ("ln1_g", "ln1_b", "ln2_g", "ln2_b"):
        put(n, i["L1_attn_" + n])
    put("lqkv", np.concatenate([i["L1_attn_wq"], i["L1_attn_wk"], i["L1_attn_wv"]], 1))
    put("lwo", i["L1_attn_wo"])
    put("cw1", i["L1_attn_cms_w1"].transpose(1, 0, 2).reshape(P, LEVELS * 512))
    put("cb1", i["L1_attn_cms_b1"].reshape(LEVELS * HC, P).T)
    put("cw2", i["L1_attn_cms_w2"].reshape(LEVELS, HC, P, P).transpose(2, 0, 1, 3).reshape(P, LEVELS * 512))
    put("cb2", i["L1_attn_cms_b2"].T)
    put("cb2row", i["L1_attn_cms_b2"][LEVELS - 1][None])
    return a


def pack_late(i):
    a = np.zeros((P, LATE_N), np.float32)

    def put(name, v, row=0):
        s, z = LATE_AT[name]
        a[row:row + v.shape[0], s:s + v.shape[1]] = v

    f = {n[len("L1_ffn_"):]: v for n, v in i.items() if n.startswith("L1_ffn_")}
    everywhere = lambda v: np.broadcast_to(v, (P, v.shape[-1]))
    put("lident", np.eye(P, dtype=np.float32))
    put("iota", everywhere(np.arange(EXPERTS, dtype=np.float32)))
    put("g1x", np.concatenate([f["shared_w1"][:P], f["halt_w1"]], 1))
    put("g1v", f["shared_w1"][P:])
    put("g1b", np.concatenate([f["shared_b1"], f["halt_b1"]])[:, None])
    put("ew1x", f["expert_w1"][:, :P].transpose(1, 0, 2).reshape(P, 512))
    put("ew1v", f["expert_w1"][:, P:].transpose(1, 0, 2).reshape(P, 512))
    put("eb1", f["expert_b1"].reshape(HC, P).T)
    put("rw1", f["router_w1"])
    put("rb1", f["router_b1"][:, None])
    put("rw2", f["router_w2"])
    put("rb2", everywhere(f["router_b2"]))
    put("sw2", f["shared_w2"])
    put("hw2", np.broadcast_to(f["halt_w2"], (HHID, P)), EHID)
    put("hb2", np.broadcast_to(f["halt_b2"], (P, 1)))
    put("ew2", f["expert_w2"].reshape(HC, P, 384).transpose(1, 0, 2).reshape(P, 4 * 384))
    for g in (0, 32, 64):
        put("eb2", f["expert_b2"], g)
        put("sb2", np.broadcast_to(f["shared_b2"], (EXPERTS, 384)), g)
    put("mu", f["mu"][:, None])
    put("shw", np.broadcast_to(f["shared_weight"], (P, 1)))
    put("esel", np.kron(np.eye(EXPERTS, dtype=np.float32), np.ones((1, EHID), np.float32)))
    put("fw1", f["refine_w1"])
    put("fb1", f["refine_b1"].reshape(2, P).T)
    put("fw2", f["refine_w2"].reshape(2, P, P).transpose(1, 0, 2).reshape(P, 256))
    put("fb2row", everywhere(f["refine_b2"]))
    put("iwrow", everywhere(f["integration_weight"]))
    return a


def kernel(**inputs):
    import numpy as _np
    import concourse.bacc as _bacc
    from concourse.bass_utils import run_bass_kernel_spmd as _run

    i = {n: _np.asarray(v) for n, v in inputs.items()}
    arrays = {"x": i["L0_attn_x"].reshape(NSEQ * SEQ, P), "early": pack_early(i), "late": pack_late(i)}
    nc = _bacc.Bacc("TRN2", target_bir_lowering=False, num_devices=1)
    aps = [nc.dram_tensor(n, a.shape, F32, kind="ExternalInput").ap() for n, a in arrays.items()]
    out = nc.dram_tensor("out", (NSEQ * SEQ, P), F32, kind="ExternalOutput").ap()
    build(nc, *aps, out)
    r = _run(nc, [arrays], core_ids=[0])
    return r.results[0]["out"].reshape(NSEQ, SEQ, P)
```

```python
import numpy as np
import concourse.bass as bass
from concourse import mybir
from contextlib import ExitStack

F32 = mybir.dt.float32
F32R = mybir.dt.float32r
BF16 = mybir.dt.bfloat16
U32 = mybir.dt.uint32
ALU = mybir.AluOpType
ACT = mybir.ActivationFunctionType
AXX = mybir.AxisListType.X

P = 128
SEQ = 512
NSEQ = 8
TILES = SEQ // P
NT = NSEQ * TILES
HEADS, HD = 16, 8
LEVELS = 3
HC = 4
EXPERTS = 8
EHID = 64
HHID = 32
LN_EPS = 1e-5
NORM_EPS = 1e-12

EARLY = [
    ("ident", 128), ("wqkv", 384), ("bqkv", 384), ("tril", 128), ("blockdiag", 128),
    ("w1", 128), ("b1", 1), ("w2", 512), ("b2", 4), ("w3", 512), ("b3", 128),
    ("wr", 128), ("wk", 128), ("wv", 128), ("mu_r", 1), ("mu_k", 1),
    ("ln1_g", 1), ("ln1_b", 1), ("lqkv", 384), ("lwo", 128), ("ln2_g", 1), ("ln2_b", 1),
    ("cb1", LEVELS * 4), ("cw1", LEVELS * 512), ("cw2", LEVELS * 512), ("cb2", LEVELS), ("cb2row", 128),
]
LATE = [
    ("lident", 128), ("iota", 8),
    ("g1x", 96), ("g1v", 96), ("g1b", 1), ("ew1x", 512), ("ew1v", 512), ("eb1", 4),
    ("rw1", 128), ("rb1", 1), ("rw2", 8), ("rb2", 8),
    ("sw2", 384), ("hw2", 128), ("hb2", 1), ("ew2", 4 * 384), ("eb2", 384), ("sb2", 384),
    ("mu", 1), ("shw", 1), ("esel", 512), ("csel", 128),
    ("fw1", 256), ("fb1", 2), ("fw2", 256), ("fb2row", 128), ("iwrow", 128),
]


PASSES = ((0, 0), (1, 0), (0, 1))


def columns(table):
    at, out = 0, {}
    for name, n in table:
        out[name] = (at, at + n)
        at += n
    return out, at


EARLY_AT, EARLY_N = columns(EARLY)
FIRST_N = EARLY_AT["bqkv"][1]
LATE_AT, LATE_N = columns(LATE)

SEMAPHORES = """
w_first w_early w_late x_in0 x_in1 x_in2 x_in3 out_done
st_a0 st_a1 st_a2 st_a3 st_a4 st_b st_c ln_var ln_sd ln_rs
var_half sd_half rs_half a1_xc a1_xn a1_tr a1_xt a1_mm a1_ev a1_sq a1_nrm a1_max a1_rn
a2_qk a2_xb a2_tq a2_tk a2_qT a2_kT a2_s a2_E a2_o a2_rc a2_on a2_to a2_oT a2_w1 a2_h1 a2_w2 a2_h2 a2_w3 a2_x
b_om b_xc b_xn b_tr b_xT b_tk b_xr b_xk b_r b_k b_rs b_kr b_ka b_o b_ot b_x
c1_x1 c1_hn c1_tr c1_hT c1_mm c1_tok c1_q c1_qT c1_m c1_M c1_kv c1_in c1_qm c1_red c1_yin c1_y c1_ty c1_yT c1_wo c1_xp
c3_wh c3_xc c3_xn c3_xa c3_xb c3_tr c3_hT c3_h c3_uhi c3_w1 c3_g c3_lo c3_w2 c3_w2e
k_sw k_dve k_sets k_iw
d0_xc d0_xn d0_xa d0_xb d0_tr d0_xi d0_r d0_rh d0_l d0_lg d0_mx d0_ix d0_if d0_d d0_th d0_cw d0_ot d0_oh1 d0_oh2
""".split() + [f"d_{n}" for n in
                "wh xh vh xs C g ge m hm u ev ex ln sp xm t1 t2 vn U gU Va Vs Da Ds hv hx v v2 x".split()] + \
    "e_1 e_g e_2 e_t e_x".split()


UNITS = {
    1: [("b", 0, 4), ("b", 1, 5), ("b", 2, 6), ("g", 0, 7), ("g", 1, 4), ("g", 2, 5), ("h", 0, 6)],
    2: [("b", 0, 4), ("b", 1, 5), ("b", 2, 6), ("a", 0, 7), ("a", 1, 4), ("a", 2, 5), ("g", 0, 6), ("g", 1, 7),
        ("g", 2, 4), ("h", 0, 5)],
}
NU = {it: len(u) for it, u in UNITS.items()}
U0 = {1: 0, 2: NU[1] * NSEQ}


def need(eng, sem, value):
    if not isinstance(value, int) or value > 0:
        eng.wait_ge(sem, value)


def settle(eng, S):
    eng.wait_ge(S["x_in0"], 16)


def pairs(eng, body):
    body(0)
    with eng.Fori(1, NSEQ // 2) as pair:
        body(pair * 2)


def pairs_ends(eng, body):
    body(0)
    with eng.Fori(1, NSEQ // 2 - 1) as pair:
        body(pair * 2)
    body(NSEQ - 2)


MOST, LAST = slice(0, NT - 2 * TILES), slice(NT - 2 * TILES, NT)


def build(nc, x, early, late, out):
    with ExitStack() as ctx:
        S = {n: ctx.enter_context(nc.semaphore(n)) for n in SEMAPHORES}

        def sb(name, shape, dt=F32):
            return ctx.enter_context(nc.sbuf_tensor(name, shape, dt))

        PS = ctx.enter_context(nc.psum_tensor("PS", [P, 8, 512], F32))
        X = sb("X", [P, NT, P])
        MV = sb("MV", [P, 2, NT, 2])
        RS = sb("RS", [P, 2, NT])
        SD = sb("SD", [P, NT])
        small = sb("small", [P, 512])
        WL = sb("WL", [P, LATE_N])
        KEEP_N, TEMP_N = 20350, 22200
        with nc.sbuf_tensor("KEEP_R", [P, KEEP_N], F32R) as KEEP_R, nc.sbuf_tensor("TEMP_R", [P, TEMP_N], F32R) as TEMP_R:
            pass
        KEEP = sb("KEEP", [P, KEEP_N])
        TEMP = sb("TEMP", [P, TEMP_N])

        def cut(region, at):
            pos = [at]

            def take(*shape):
                n = int(np.prod(shape))
                ap = region[:, pos[0]:pos[0] + n]
                pos[0] += n
                assert pos[0] <= region.shape[1], (pos[0], region.shape)
                if len(shape) == 2:
                    ap = ap.rearrange("p (a b) -> p a b", a=shape[0])
                elif len(shape) == 4:
                    ap = ap.rearrange("p (a b c d) -> p a b c d", a=shape[0], b=shape[1], c=shape[2])
                elif len(shape) == 3:
                    ap = ap.rearrange("p (a b c) -> p a b c", a=shape[0], b=shape[1])
                return ap
            return take

        WE = TEMP[:, 0:EARLY_N]

        def we(name):
            a, z = EARLY_AT[name]
            return WE[:, a:z]

        def wl(name):
            a, z = LATE_AT[name]
            return WL[:, a:z]

        ident = we("ident")
        sm = cut(small, 0)
        stat = sm(2, TILES, 6)
        mvt = sm(2, TILES, 2)
        ssq = sm(NT, 2)
        rnorm = sm(NT, 2)
        recip = sm(2, TILES)
        om_r, om_k = sm(1), sm(1)
        v1 = sm(NT)
        rs2 = sm(NT)
        nmr = sm(NT)
        hb2h = sm(1)

        def tiles(ap, t):
            return ap[:, bass.ds(t * TILES, TILES)]

        def bc(ap, n=P):
            return ap.unsqueeze(2).to_broadcast([P, ap.shape[1], n])

        def rows(ap, n=TILES):
            return ap.unsqueeze(1).to_broadcast([P, n, ap.shape[1]])

        ka = cut(KEEP, 0)
        QKV = ka(NT, 3, 132)
        xn, xT = ka(2, TILES, P), ka(2, SEQ)
        xc = ka(2, TILES, P)
        ta = cut(TEMP, EARLY_N)
        qn, kn = ta(2, TILES, P), ta(2, TILES, P)
        qT, kT = ta(2, SEQ), ta(2, SEQ)
        E = ta(2, 4 * SEQ)
        on, oT = ta(2, TILES, P), ta(2, SEQ)
        h1 = ta(2, SEQ)
        h2 = ta(2, HC * SEQ)
        junk = ka(4, P)
        kb = cut(KEEP, 0)
        b_xn, b_xc, b_tr, b_tk = kb(2, TILES, P), kb(2, TILES, P), kb(2, SEQ), kb(2, SEQ)
        b_xT = kb(2, SEQ + 4)
        b_xr, b_xk, b_rs, b_kr, b_ka, b_ot = [kb(2, SEQ) for _ in range(6)]
        kc = cut(KEEP, 0)
        XP = kc(NT, P)
        c_hn, c_hT, c_qT, c_y, c_yT = kc(2, TILES, P), kc(2, SEQ), kc(2, SEQ), kc(2, TILES, P), kc(2, SEQ)
        tok = kc(2, TILES, 384)
        kv = kc(2, 1024)
        tc = cut(TEMP, EARLY_N)
        qm = tc(2, 1024)
        Mbd = tc(2, 3, P)
        kd = cut(KEEP, NT * P)
        d_xc, d_xn, d_hT = kd(2, TILES, P), kd(2, TILES, P), kd(2, SEQ)
        d_G = kd(2, HC * SEQ)
        kdr = cut(TEMP_R, EARLY_N)
        hTr = kdr(2, 2, SEQ)
        Gr = kdr(2, 2, HC * SEQ)
        CW_AT, CW_N = EARLY_AT["cw1"][0], LEVELS * 512 + (LEVELS - 1) * 512
        CWr = kdr(2, CW_N)

        ke = cut(KEEP, 0)
        XI, VS = ke(NSEQ * SEQ), ke(NSEQ * SEQ)
        OH = ke(2, NSEQ * SEQ // 2).bitcast(BF16)
        kr = cut(KEEP_R, 3 * NSEQ * SEQ)
        W1_AT, W1_N = LATE_AT["g1x"][0], LATE_AT["ew1v"][1] - LATE_AT["g1x"][0]
        W1 = kr(2, W1_N)
        XVS = kr(2, 2, 2, SEQ)

        def w1(name, part):
            a, z = LATE_AT[name]
            return W1[:, part, a - W1_AT:z - W1_AT]
        te = cut(KEEP, 3 * NSEQ * SEQ + 2 * W1_N + 8 * SEQ)
        esel, eyeb, csel = te(256).bitcast(BF16), te(64).bitcast(BF16), te(64).bitcast(BF16)
        bias2 = te(2, 192).bitcast(BF16)
        swc, hosw, nhosw = te(1), te(1), te(1)
        fbiw = te(P)
        tf = cut(TEMP, 4096)
        e_xc, e_xn = tf(2, TILES, P), tf(2, TILES, P)
        e_rh = tf(2, SEQ)
        oht = tf(2 * NT * 48).bitcast(BF16).rearrange("p (e n g r) -> p e n g r", e=2, n=NT, g=3)
        lg, m8, ixf = tf(2, TILES, 8), tf(2, TILES, 8), tf(NT, 2)
        ix = tf(2, TILES * 8).bitcast(U32)
        dd, th = tf(NT), tf(NT)
        cw, cwr = tf(2, NT), tf(2, NT)
        tw = cut(KEEP, 3 * NSEQ * SEQ + 2 * W1_N + 2)
        r1, r2 = tw(768), tw(768)
        p0, p1 = tw(384).bitcast(BF16), tw(384).bitcast(BF16)
        tg_ = cut(TEMP, 1024)
        hs = tg_(2, SEQ)
        hE = tg_(HC, SEQ)
        hM = tg_(2, 2, HC * SEQ)
        az, rz, ta_, tgt = tg_(3, SEQ), tg_(3, SEQ), tg_(3, SEQ), tg_(3, SEQ)
        xm, hlt = tg_(SEQ), tg_(SEQ)
        vsum, dsum = tg_(SEQ), tg_(SEQ)
        th_ = cut(TEMP, 1024)
        rf = th_(2, 2 * SEQ)
        ot = th_(2, SEQ)

        def seq(ap, t):
            return ap[:, bass.ds(t * SEQ, SEQ)]

        ones_col = QKV[:, :, 2, 128:129]
        x_in = x.rearrange("(n j p) d -> n p j d", j=2 * TILES, p=P)
        x_out = out.rearrange("(n j p) d -> n p j d", j=TILES, p=P)
        block = ctx.enter_context(nc.Block())

        @block.sync
        def _(sp):
            for t in range(NSEQ // 2):
                sp.dma_start(X[:, 2 * t * TILES:2 * (t + 1) * TILES, :], x_in[t]).then_inc(S[f"x_in{t}"], 16)
            sp.dma_start(WE[:, FIRST_N:], early[:, FIRST_N:]).then_inc(S["w_early"], 16)
            sp.dma_start(WL[:, :], late).then_inc(S["w_late"], 16)
            for t in range(NSEQ):
                sp.wait_ge(S["e_x"], t + 1)
                sp.dma_start(x_out[t], X[:, t * TILES:(t + 1) * TILES, :]).then_inc(S["out_done"], 16)
            sp.wait_ge(S["out_done"], 16 * NSEQ)

        @block.gpsimd
        def _(pool):
            def normed(t, k, src, n, cen, dst, sc, sn):
                pool.tensor_tensor(cen[:, k], tiles(src, t), bc(tiles(MV[:, n, :, 0], t)), ALU.subtract).then_inc(sc, 1)
                pool.wait_ge(sc, t + 1)
                pool.tensor_tensor(dst[:, k], cen[:, k], bc(tiles(RS[:, n, :], t)), ALU.mult).then_inc(sn, 1)

            pool.wait_ge(S["rs_half"], 1)

            def a1(b):
                for k in (0, 1):
                    need(pool, S["a1_tr"], b + k - 1)
                    normed(b + k, k, X, 0, xc, xn, S["a1_xc"], S["a1_xn"])
            a1(0)
            a1(2)
            pool.wait_ge(S["ln_rs"], 1)
            with pool.Fori(2, NSEQ // 2) as pair:
                a1(pair * 2)

            pool.wait_ge(S["a1_rn"], 1)
            pool.wait_ge(S["w_early"], 16)

            def a2(b):
                for k in (0, 1):
                    t = b + k
                    need(pool, S["a2_tk"], t - 1)
                    pool.tensor_tensor(qn[:, k], tiles(QKV[:, :, 0, 0:P], t), bc(tiles(rnorm[:, :, 0], t)), ALU.mult)\
                        .then_inc(S["a2_qk"], 1)
                    pool.tensor_tensor(kn[:, k], tiles(QKV[:, :, 1, 0:P], t), bc(tiles(rnorm[:, :, 1], t)), ALU.mult)\
                        .then_inc(S["a2_qk"], 1)
                    pool.tensor_tensor(tiles(X, t), tiles(X, t), rows(we("b3")), ALU.add).then_inc(S["a2_xb"], 1)
            a2(0)
            with pool.Fori(1, NSEQ // 2 - 1) as pair:
                a2(pair * 2)
            pool.wait_ge(S["a1_rn"], 2)
            a2(NSEQ - 2)

            pool.wait_ge(S["ln_rs"], 2)

            def b_(b):
                for k in (0, 1):
                    need(pool, S["b_tr"], b + k - 1)
                    normed(b + k, k, X, 1, b_xc, b_xn, S["b_xc"], S["b_xn"])
                for k in (0, 1):
                    t = b + k
                    pool.wait_ge(S["b_kr"], t + 1)
                    need(pool, S["b_o"], t - 1)
                    pool.tensor_tensor(b_ka[:, k], b_kr[:, k], b_kr[:, k], ALU.mult).then_inc(S["b_ka"], 1)
            pairs(pool, b_)

            pool.wait_ge(S["ln_rs"], 3)

            def hn(t, k):
                pool.wait_ge(S["c1_x1"], 4 * t + 4)
                need(pool, S["c1_tr"], t - 1)
                pool.tensor_tensor(c_hn[:, k], tiles(XP, t), bc(tiles(rs2, t)), ALU.mult).then_inc(S["c1_hn"], 1)

            def kvs(t, k):
                for c in range(TILES):
                    pool.wait_ge(S["c1_tok"], 4 * t + c + 1)
                    need(pool, S["c1_in"], 4 * t + c - 1)
                    o = kv[:, c % 2].rearrange("p (h v k) -> p h v k", h=HEADS, v=HD)
                    kk = tok[:, k, c, P:2 * P].rearrange("p (h o k) -> p h o k", h=HEADS, o=1).to_broadcast([P, HEADS, HD, HD])
                    vv = tok[:, k, c, 2 * P:3 * P].rearrange("p (h v o) -> p h v o", h=HEADS, o=1).to_broadcast([P, HEADS, HD, HD])
                    pool.tensor_tensor(o, kk, vv, ALU.mult).then_inc(S["c1_kv"], 1)

            hn(0, 0)
            hn(1, 1)

            def c1(b):
                for k in (0, 1):
                    kvs(b + k, k)
                    if not isinstance(b, int) or b + k + 2 < NSEQ:
                        hn(b + k + 2, k)
            pairs_ends(pool, c1)

            flat = WE[:, CW_AT:CW_AT + CW_N]
            pool.tensor_copy(CWr[:, 0], flat).then_inc(S["c3_wh"], 1)
            pool.wait_ge(S["c3_wh"], 1)
            pool.tensor_tensor(CWr[:, 1], flat, CWr[:, 0].bitcast(F32), ALU.subtract).then_inc(S["c3_wh"], 1)
            pool.wait_ge(S["ln_rs"], 4)

            def c3(b):
                for k in (0, 1):
                    t = b + k
                    need(pool, S["c3_tr"], t - 1)
                    normed(t, k, XP, 1, d_xc, d_xn, S["c3_xc"], S["c3_xn"])
                for k in (0, 1):
                    t = b + k
                    pool.wait_ge(S["c3_hT"], t + 1)
                    pool.tensor_tensor(hTr[:, k, 1], d_hT[:, k], hTr[:, k, 0].bitcast(F32), ALU.subtract).then_inc(S["c3_h"], 1)
                for k in (0, 1):
                    t = b + k
                    pool.tensor_tensor(tiles(X, t), tiles(X, t), tiles(XP, t), ALU.add).then_inc(S["c3_xa"], 1)
                    settle(pool, S)
                    pool.wait_ge(S["c3_xa"], t + 1)
                    pool.tensor_tensor(tiles(X, t), tiles(X, t), rows(we("cb2row")), ALU.add).then_inc(S["c3_xb"], 1)
            pairs(pool, c3)

            pool.wait_ge(S["w_late"], 16)
            flat = WL[:, W1_AT:W1_AT + W1_N]
            pool.tensor_copy(W1[:, 0], flat).then_inc(S["d_wh"], 1)
            pool.wait_ge(S["d_wh"], 1)
            pool.tensor_tensor(W1[:, 1], flat, W1[:, 0].bitcast(F32), ALU.subtract).then_inc(S["d_wh"], 1)

            pool.wait_ge(S["ln_rs"], 5)

            def d0(b):
                for k in (0, 1):
                    t = b + k
                    need(pool, S["d0_tr"], t - 1)
                    need(pool, S["d0_xa"], t - 1)
                    normed(t, k, X, 0, e_xc, e_xn, S["d0_xc"], S["d0_xn"])
            pairs(pool, d0)
            pool.memset(oht, 0.0).then_inc(S["d_wh"], 1)

            def halves(t, k, velocity, n):
                states, high = ([XI, VS], S["d_vh"]) if velocity else ([XI], S["d_xh"])
                need(pool, S["d_g"], 5 * (n - 1))
                settle(pool, S)
                if velocity:
                    pool.wait_ge(S["d_x"], t + 1)
                    pool.wait_ge(S["d_v"], t + 1)
                else:
                    pool.wait_ge(S["d0_xi"], t + 1)
                for i, a in enumerate(states):
                    last = pool.tensor_copy(XVS[:, k, i, 0], seq(a, t))
                last.then_inc(high, 1)
                settle(pool, S)
                pool.wait_ge(high, t + 1)
                for i, a in enumerate(states):
                    last = pool.tensor_tensor(XVS[:, k, i, 1], seq(a, t), XVS[:, k, i, 0].bitcast(F32), ALU.subtract)
                last.then_inc(S["d_xs"], 1)

            def iterate(it):
                z = NSEQ * (it - 1)
                s = lambda n: S[f"d_{n}"]

                def body(b):
                    for k in (0, 1):
                        t = b + k
                        if not isinstance(t, int) or t + 2 < NSEQ:
                            halves(t + 2, k, it == 2, t + z + 2)
                        elif it == 1:
                            halves(t + 2 - NSEQ, k, True, t + 2)
                        pool.wait_ge(s("ln"), (t + z) + 1)
                        pool.tensor_tensor(rz, az, rz, ALU.add).then_inc(s("sp"), 1)
                        if it == 1:
                            settle(pool, S)
                            pool.wait_ge(S["d0_xa"], t + 1)
                            pool.tensor_tensor(tiles(X, t), tiles(X, t), rows(fbiw), ALU.add).then_inc(S["d0_xb"], 1)
                        pool.wait_ge(s("U"), 2 * (t + z) + 2)
                        pool.tensor_tensor(vsum, rz[:, 0], rz[:, 1], ALU.add).then_inc(s("Va"), 1)
                        pool.wait_ge(s("Va"), (t + z) + 1)
                        pool.tensor_tensor(vsum, vsum, rz[:, 2], ALU.add).then_inc(s("Vs"), 1)
                pairs_ends(pool, body)
            halves(0, 0, False, 0)
            halves(1, 1, False, 1)
            pool.wait_ge(S["k_iw"], 1)
            iterate(1)
            iterate(2)

        @block.vector
        def _(dve):
            def all_stats(t, k, src, n, done):
                read, done_tiles = S[f"st_a{done // NSEQ}"], S["st_b"]
                for j in range(TILES):
                    last = dve.bn_stats(stat[:, k, j], src[:, bass.ds(t * TILES + j, 1), :].rearrange("p a d -> p (a d)"))
                last.then_inc(read, 1)
                settle(dve, S)
                dve.wait_ge(read, t + 1)
                for j in range(TILES):
                    last = dve.bn_aggr(mvt[:, k, j], stat[:, k, j])
                last.then_inc(done_tiles, 1)
                dve.wait_ge(done_tiles, done + t + 1)
                dve.tensor_copy(tiles(MV[:, n], t), mvt[:, k]).then_inc(S["st_c"], 1)

            def finish_ln(n, count, done):
                dve.wait_ge(S["st_c"], done)
                dve.tensor_scalar(v1, MV[:, n, :, 1], LN_EPS, None, ALU.add).then_inc(S["ln_var"], 1)
                dve.wait_ge(S["ln_sd"], count)
                dve.reciprocal(RS[:, n, :], SD[:, :]).then_inc(S["ln_rs" if count != 2 else "b_om"], 1)

            dve.memset(ones_col, 1.0)
            half = NT // 2
            for t in range(NSEQ):
                dve.wait_ge(S[f"x_in{t // 2}"], 16)
                all_stats(t, t % 2, X, 0, 0)
                if t % (NSEQ // 2) == NSEQ // 2 - 1:
                    h = slice(0, half) if t < NSEQ // 2 else slice(half, NT)
                    dve.wait_ge(S["st_c"], t + 1)
                    dve.tensor_scalar(v1[:, h], MV[:, 0, h, 1], LN_EPS, None, ALU.add).then_inc(S["var_half"], 1)
                    dve.wait_ge(S["sd_half"], 1 if t < NSEQ // 2 else 2)
                    dve.reciprocal(RS[:, 0, h], SD[:, h]).then_inc(S["rs_half" if t < NSEQ // 2 else "ln_rs"], 1)

            dve.wait_ge(S["w_first"], 16)

            def a1(b):
                for k in (0, 1):
                    for j in range(TILES):
                        n = 4 * (b + k) + j
                        dve.wait_ge(S["a1_mm"], n + 1)
                        dve.tensor_tensor(QKV[:, bass.ds(n, 1), :, 0:P].rearrange("p a c d -> p (a c) d"),
                                          PS[:, 2 + j, 0:384].rearrange("p (c d) -> p c d", c=3),
                                          we("bqkv").rearrange("p (c d) -> p c d", c=3), ALU.add).then_inc(S["a1_ev"], 1)
            pairs(dve, a1)
            for n, part in ((1, MOST), (2, LAST)):
                dve.wait_ge(S["a1_nrm"], n)
                dve.tensor_scalar(rnorm[:, part], ssq[:, part], NORM_EPS, None, ALU.max).then_inc(S["a1_max"], 1)
                dve.wait_ge(S["a1_max"], n)
                dve.reciprocal(rnorm[:, part], rnorm[:, part]).then_inc(S["a1_rn"], 1)
            dve.wait_ge(S["w_early"], 16)

            def a2(b):
                O = PS[:, 6:8, 0:258].rearrange("p a (c d) -> p a c d", c=2)
                for k in (0, 1):
                    t = b + k
                    dve.wait_ge(S["a2_o"], t + 1)
                    dve.reciprocal(recip[:, k].rearrange("p (a c) -> p a c", a=2).unsqueeze(3), O[:, :, :, 128:129]).then_inc(S["a2_rc"], 1)
                    dve.wait_ge(S["a2_rc"], t + 1)
                    need(dve, S["a2_to"], t - 1)
                    dve.tensor_tensor(on[:, k].rearrange("p (a c) d -> p a c d", a=2), O[:, :, :, 0:P],
                                      recip[:, k].rearrange("p (a c) -> p a c", a=2).unsqueeze(3).to_broadcast([P, 2, 2, P]),
                                      ALU.mult).then_inc(S["a2_on"], 1)
                for k in (0, 1):
                    t = b + k
                    dve.wait_ge(S["a2_w1"], t + 1)
                    need(dve, S["a2_w2"], 4 * (t - 1))
                    dve.tensor_scalar(h1[:, k], PS[:, 1, :], we("b1"), 0.0, ALU.add, ALU.max).then_inc(S["a2_h1"], 1)
                for k in (0, 1):
                    t = b + k
                    dve.wait_ge(S["a2_w3"], t + 1)
                    dve.wait_ge(S["a2_xb"], t + 1)
                    dve.tensor_tensor(tiles(X, t), PS[:, 0, :].rearrange("p (j d) -> p j d", j=TILES), tiles(X, t),
                                      ALU.add).then_inc(S["a2_x"], 1)
                    settle(dve, S)
                    dve.wait_ge(S["a2_x"], t + 1)
                    all_stats(t, k, X, 1, NSEQ)
            pairs(dve, a2)
            dve.memset(b_xT[:, :, 0:1], 0.0)
            dve.tensor_scalar(om_r, we("mu_r"), -1.0, 1.0, ALU.mult, ALU.add)
            dve.tensor_scalar(om_k, we("mu_k"), -1.0, 1.0, ALU.mult, ALU.add)
            finish_ln(1, 1, 2 * NSEQ)

            def b_(b):
                for k in (0, 1):
                    t = b + k
                    dve.wait_ge(S["b_tk"], t + 1)
                    need(dve, S["b_r"], t - 1)
                    dve.scalar_tensor_tensor(b_xr[:, k], b_xT[:, k, 1:SEQ + 1], we("mu_r"), b_tr[:, k], ALU.mult, ALU.add)\
                        .then_inc(S["b_xr"], 1)
                    need(dve, S["b_k"], t - 1)
                    dve.scalar_tensor_tensor(b_xk[:, k], b_xT[:, k, 1:SEQ + 1], we("mu_k"), b_tk[:, k], ALU.mult, ALU.add)\
                        .then_inc(S["b_xk"], 1)
                for k in (0, 1):
                    t = b + k
                    dve.wait_ge(S["b_o"], t + 1)
                    dve.wait_ge(S["b_rs"], t + 1)
                    need(dve, S["b_x"], t - 1)
                    dve.tensor_tensor(b_ot[:, k], PS[:, 6 + k, :], b_rs[:, k], ALU.mult).then_inc(S["b_ot"], 1)
                    dve.wait_ge(S["b_ot"], t + 1)
                    dve.tensor_tensor(tiles(X, t), b_ot[:, k].rearrange("p (j d) -> p j d", j=TILES), tiles(X, t),
                                      ALU.add).then_inc(S["b_x"], 1)
                    settle(dve, S)
                    dve.wait_ge(S["b_x"], t + 1)
                    all_stats(t, k, X, 0, 2 * NSEQ)
            pairs(dve, b_)

            finish_ln(0, 2, 3 * NSEQ)
            dve.wait_ge(S["b_om"], 1)
            dve.tensor_tensor(v1, MV[:, 0, :, 1], RS[:, 0, :], ALU.mult).then_inc(S["b_om"], 1)
            dve.wait_ge(S["b_om"], 2)
            dve.tensor_tensor(v1, v1, RS[:, 0, :], ALU.mult).then_inc(S["b_om"], 1)
            dve.wait_ge(S["b_om"], 3)
            dve.tensor_scalar(v1, v1, LN_EPS, None, ALU.add).then_inc(S["ln_var"], 1)
            dve.wait_ge(S["ln_sd"], 3)
            dve.reciprocal(rs2, SD[:, :]).then_inc(S["b_om"], 1)
            dve.scalar_tensor_tensor(nmr, MV[:, 0, :, 0], -1.0, RS[:, 0, :], ALU.mult, ALU.mult).then_inc(S["b_om"], 1)
            dve.wait_ge(S["b_om"], 5)
            dve.memset(stat[:, 0, 0, 0:1], 0.0).then_inc(S["ln_rs"], 1)

            def mask_m(t, k):
                dve.wait_ge(S["c1_m"], t + 1)
                need(dve, S["c1_yin"], t - 1)
                dve.tensor_tensor(Mbd[:, k], PS[:, 2, 0:384].rearrange("p (c d) -> p c d", c=3), rows(we("blockdiag"), 3),
                                  ALU.mult).then_inc(S["c1_M"], 1)

            def chunks(t, k):
                need(dve, S["c1_ty"], t - 1)
                for c in range(TILES):
                    dve.wait_ge(S["c1_in"], 4 * t + c + 1)
                    need(dve, S["c1_red"], 4 * t + c - 1)
                    acc = PS[:, 4 + 2 * (c % 2):6 + 2 * (c % 2), :].rearrange("p a (h v k) -> p (a h) v k", h=HEADS // 2, v=HD)
                    q = tok[:, k, c, 0:P].rearrange("p (h o k) -> p h o k", h=HEADS, o=1).to_broadcast([P, HEADS, HD, HD])
                    dve.tensor_tensor(qm[:, c % 2].rearrange("p (h v k) -> p h v k", h=HEADS, v=HD), acc, q, ALU.mult)\
                        .then_inc(S["c1_qm"], 1)
                    dve.wait_ge(S["c1_qm"], 4 * t + c + 1)
                    dve.tensor_reduce(c_y[:, k, c], qm[:, c % 2].rearrange("p (h k) -> p h k", k=HD), AXX, ALU.add)\
                        .then_inc(S["c1_red"], 1)
                dve.wait_ge(S["c1_yin"], t + 1)
                dve.wait_ge(S["c1_red"], 4 * t + 4)
                dve.tensor_tensor(c_y[:, k, 1:TILES], PS[:, 3, 0:384].rearrange("p (c d) -> p c d", c=3), c_y[:, k, 1:TILES],
                                  ALU.add).then_inc(S["c1_y"], 1)

            def residual(t, k):
                dve.wait_ge(S["c1_wo"], t + 1)
                dve.tensor_tensor(tiles(XP, t), PS[:, 2, :].rearrange("p (j d) -> p j d", j=TILES), tiles(XP, t),
                                  ALU.add).then_inc(S["c1_xp"], 1)
                settle(dve, S)
                dve.wait_ge(S["c1_xp"], t + 1)
                all_stats(t, k, XP, 1, 3 * NSEQ)

            mask_m(0, 0)

            def c1(b):
                for k in (0, 1):
                    t = b + k
                    if not isinstance(t, int) or t + 1 < NSEQ:
                        mask_m(t + 1, 1 - k)
                    chunks(t, k)
                    if not isinstance(t, int) or t > 0:
                        residual(t - 1, 1 - k)
            pairs_ends(dve, c1)
            residual(NSEQ - 1, 1)
            dve.wait_ge(S["st_c"], 4 * NSEQ)
            dve.tensor_scalar(v1, MV[:, 1, :, 1], LN_EPS, None, ALU.add).then_inc(S["ln_var"], 1)
            dve.wait_ge(S["ln_sd"], 4)
            dve.reciprocal(RS[:, 1, :], SD[:, :]).then_inc(S["ln_rs"], 1)

            dve.wait_ge(S["w_late"], 16)
            dve.tensor_copy(esel, wl("esel"))
            dve.tensor_copy(csel, wl("csel"))
            dve.tensor_copy(eyeb, wl("lident"))
            dve.tensor_tensor(fbiw, wl("fb2row"), wl("iwrow"), ALU.mult).then_inc(S["k_iw"], 1)
            both = WL[0:96, LATE_AT["eb2"][0]:LATE_AT["sb2"][1]]
            dve.tensor_copy(p0[0:96], both).then_inc(S["k_dve"], 1)
            dve.wait_ge(S["k_dve"], 1)
            dve.tensor_tensor(r1[0:96], both, p0[0:96], ALU.subtract).then_inc(S["k_dve"], 1)
            dve.wait_ge(S["k_dve"], 2)
            dve.tensor_copy(p1[0:96], r1[0:96]).then_inc(S["k_dve"], 1)
            dve.wait_ge(S["k_dve"], 3)
            dve.tensor_tensor(r2[0:96], r1[0:96], p1[0:96], ALU.subtract).then_inc(S["k_dve"], 1)
            dve.wait_ge(S["k_dve"], 4)
            flat = bias2.rearrange("p a b -> p (a b)")
            dve.tensor_copy(flat[0:32], p0[0:32])
            dve.tensor_copy(flat[32:64], p1[32:64])
            dve.tensor_copy(flat[64:96], r2[64:96])
            dve.wait_ge(S["k_sw"], 1)
            dve.tensor_scalar(hosw, swc, -0.25, 0.25, ALU.mult, ALU.add)
            dve.tensor_scalar(nhosw, swc, 0.25, -0.25, ALU.mult, ALU.add).then_inc(S["k_dve"], 1)
            dve.wait_ge(S["k_dve"], 5)
            dve.tensor_scalar(swc, swc, 0.5, 0.5, ALU.mult, ALU.add).then_inc(S["k_sets"], 1)
            dve.wait_ge(S["k_sets"], 1)

            def c3(b):
                for lev in range(LEVELS):
                    if lev < LEVELS - 1:
                        for k in (0, 1):
                            for c in range(HC):
                                dve.wait_ge(S["c3_g"], 12 * b + 8 * lev + 4 * k + c + 1)
                                dve.tensor_tensor(Gr[:, k, 1, SEQ * c:SEQ * (c + 1)], d_G[:, k, SEQ * c:SEQ * (c + 1)],
                                                  Gr[:, k, 0, SEQ * c:SEQ * (c + 1)].bitcast(F32), ALU.subtract)\
                                    .then_inc(S["c3_lo"], 1)
                    for k in (0, 1):
                        t = b + k
                        dve.wait_ge(S["c3_w2"], 3 * b + 2 * lev + k + 1)
                        if lev < LEVELS - 1:
                            dve.tensor_scalar(hTr[:, k, 0], PS[:, 6 + k, :], we("cb2")[:, lev:lev + 1], None, ALU.add)\
                                .then_inc(S["c3_uhi"], 1)
                            dve.wait_ge(S["c3_uhi"], 2 * b + 2 * lev + k + 1)
                            dve.scalar_tensor_tensor(hTr[:, k, 1], PS[:, 6 + k, :], we("cb2")[:, lev:lev + 1],
                                                     hTr[:, k, 0].bitcast(F32), ALU.add, ALU.subtract).then_inc(S["c3_w2e"], 1)
                        else:
                            dve.wait_ge(S["c3_xb"], t + 1)
                            dve.tensor_tensor(tiles(X, t), PS[:, 6 + k, :].rearrange("p (j d) -> p j d", j=TILES),
                                              tiles(X, t), ALU.add).then_inc(S["c3_w2e"], 1)
                            settle(dve, S)
                            dve.wait_ge(S["c3_w2e"], 3 * b + 2 * lev + k + 1)
                            all_stats(t, k, X, 0, 4 * NSEQ)
            pairs(dve, c3)
            dve.wait_ge(S["st_c"], 5 * NSEQ)
            dve.tensor_scalar(v1, MV[:, 0, :, 1], LN_EPS, None, ALU.add).then_inc(S["ln_var"], 1)
            dve.wait_ge(S["ln_sd"], 5)
            dve.reciprocal(RS[:, 0, :], SD[:, :]).then_inc(S["ln_rs"], 1)

            def d0(b):
                for k in (0, 1):
                    t = b + k
                    dve.wait_ge(S["d0_xn"], t + 1)
                    dve.tensor_tensor(tiles(X, t), tiles(X, t), e_xn[:, k], ALU.add).then_inc(S["d0_xa"], 1)
                for k in (0, 1):
                    t = b + k
                    dve.wait_ge(S["d0_l"], t + 1)
                    dve.tensor_tensor(lg[:, k], PS[:, 4 + k, 0:32].rearrange("p (j e) -> p j e", j=TILES), rows(wl("rb2")), ALU.add)\
                        .then_inc(S["d0_lg"], 1)
                    settle(dve, S)
                    dve.wait_ge(S["d0_lg"], t + 1)
                    for j in range(TILES):
                        last = dve.max(m8[:, k, j], lg[:, k, j])
                    last.then_inc(S["d0_mx"], 1)
                    settle(dve, S)
                    dve.wait_ge(S["d0_mx"], t + 1)
                    for j in range(TILES):
                        last = dve.max_index(ix[:, k, 8 * j:8 * j + 8], m8[:, k, j], lg[:, k, j])
                    last.then_inc(S["d0_ix"], 1)
                    dve.tensor_tensor(tiles(dd, t), m8[:, k, :, 0], m8[:, k, :, 1], ALU.subtract).then_inc(S["d0_d"], 1)
                    dve.wait_ge(S["d0_ix"], t + 1)
                    dve.tensor_copy(tiles(ixf, t), ix[:, k].rearrange("p (j e) -> p j e", j=TILES)[:, :, 0:2]).then_inc(S["d0_if"], 1)
            pairs(dve, d0)

            dve.wait_ge(S["d0_if"], NSEQ)
            dve.wait_ge(S["d_wh"], 3)
            for e in (0, 1):
                dve.tensor_tensor(oht[:, e, :, :, 0:EXPERTS], wl("iota").unsqueeze(1).unsqueeze(1).to_broadcast([P, NT, 3, EXPERTS]),
                                  ixf[:, :, e:e + 1].unsqueeze(2).to_broadcast([P, NT, 3, EXPERTS]), ALU.is_equal)
            dve.wait_ge(S["d0_th"], 1)
            dve.tensor_scalar(cw[:, 0], th, 1.0, hosw, ALU.add, ALU.mult)
            dve.tensor_scalar(cw[:, 1], th, -1.0, nhosw, ALU.add, ALU.mult).then_inc(S["d0_cw"], 1)
            part = lambda g: oht[:, :, :, g, EXPERTS]
            dve.wait_ge(S["d0_cw"], 1)
            dve.tensor_copy(part(0), cw).then_inc(S["d0_cw"], 1)
            dve.wait_ge(S["d0_cw"], 2)
            dve.tensor_tensor(cwr, cw, part(0), ALU.subtract).then_inc(S["d0_cw"], 1)
            dve.wait_ge(S["d0_cw"], 3)
            dve.tensor_copy(part(1), cwr).then_inc(S["d0_cw"], 1)
            dve.wait_ge(S["d0_cw"], 4)
            dve.tensor_tensor(part(2), cwr, part(1), ALU.subtract).then_inc(S["d0_cw"], 1)

            def rows_out(b):
                for k in (0, 1):
                    t = b + k
                    dve.wait_ge(S["d0_ot"], t + 1)
                    dve.tensor_copy(OH[0:96, 0, bass.ds(t * SEQ, SEQ)], PS[0:96, 4 + 2 * k, 0:256].bitcast(BF16))\
                        .then_inc(S["d0_oh1"], 1)
            pairs(dve, rows_out)

            def iterate(it):
                z = NSEQ * (it - 1)
                s = lambda n: S[f"d_{n}"]

                def masks(t, k):
                    need(dve, s("u"), U0[it] + NU[it] * (t - 1))
                    for c in range(HC):
                        dve.wait_ge(s("m"), 4 * (t + z) + c + 1)
                        dve.wait_ge(s("ge"), 5 * (t + z) + c + 2)
                        for e in (0, 1):
                            dve.tensor_tensor(hM[:, k, e, SEQ * c:SEQ * (c + 1)], hE[:, c], PS[:, 2 + e, :], ALU.mult)\
                                .then_inc(s("hm"), 1)

                def step(t):
                    dve.tensor_scalar(xm, seq(XI, t), wl("mu"), None, ALU.subtract).then_inc(s("xm"), 1)
                    dve.wait_ge(s("xm"), (t + z) + 1)
                    three = lambda ap: ap.unsqueeze(1).to_broadcast([P, 3, SEQ])
                    dve.wait_ge(s("sp"), (t + z) + 1)
                    dve.tensor_tensor(rz, rz, three(xm), ALU.mult).then_inc(s("t1"), 1)
                    dve.wait_ge(s("t1"), (t + z) + 1)
                    if it == 2:
                        dve.wait_ge(s("ev"), U0[it] + NU[it] * t + NU[it])
                        dve.scalar_tensor_tensor(ta_, ta_, 1.0, three(seq(VS, t)), ALU.add, ALU.mult).then_inc(s("t2"), 1)
                        dve.wait_ge(s("t2"), t + 1)
                        dve.scalar_tensor_tensor(rz, ta_, 0.5, rz, ALU.mult, ALU.subtract).then_inc(s("vn"), 1)
                        dve.wait_ge(s("vn"), t + 1)
                    dve.tensor_scalar(rz[:, 0], rz[:, 0], swc, None, ALU.mult).then_inc(s("U"), 1)
                    dve.wait_ge(s("C"), (t + z) + 1)
                    dve.tensor_tensor(rz[:, 1:3], rz[:, 1:3], PS[:, 2:4, :], ALU.mult).then_inc(s("U"), 1)
                    dve.wait_ge(s("U"), 2 * (t + z) + 2)
                    dve.wait_ge(s("ev"), U0[it] + NU[it] * t + NU[it])
                    dve.scalar_tensor_tensor(tgt, tgt, 1.0, rz, ALU.add, ALU.mult).then_inc(s("gU"), 1)
                    dve.wait_ge(s("gU"), (t + z) + 1)
                    dve.tensor_tensor(dsum, tgt[:, 0], tgt[:, 1], ALU.add).then_inc(s("Da"), 1)
                    dve.wait_ge(s("Da"), (t + z) + 1)
                    dve.tensor_tensor(dsum, dsum, tgt[:, 2], ALU.add).then_inc(s("Ds"), 1)
                    dve.wait_ge(s("Ds"), (t + z) + 1)
                    sign = -1.0 if it == 1 else 1.0
                    dve.scalar_tensor_tensor(dsum, hlt, 1.0, dsum, ALU.add, ALU.mult).then_inc(s("hx"), 1)
                    dve.wait_ge(s("Vs"), (t + z) + 1)
                    if it == 2:
                        dve.tensor_tensor(vsum, vsum, seq(VS, t), ALU.subtract).then_inc(s("v2"), 1)
                        dve.wait_ge(s("v2"), t + 1)
                    dve.scalar_tensor_tensor(vsum, hlt, 1.0, vsum, ALU.add, ALU.mult).then_inc(s("hv"), 1)
                    dve.wait_ge(s("hx"), (t + z) + 1)
                    dve.scalar_tensor_tensor(seq(XI, t), dsum, sign * 0.1 * 0.5 * 0.5, seq(XI, t), ALU.mult, ALU.add)\
                        .then_inc(s("x"), 1)
                    dve.wait_ge(s("hv"), (t + z) + 1)
                    if it == 2:
                        dve.scalar_tensor_tensor(seq(VS, t), vsum, 0.5, seq(VS, t), ALU.mult, ALU.add).then_inc(s("v"), 1)
                        dve.wait_ge(s("v"), NSEQ + t + 1)
                    else:
                        dve.tensor_scalar(seq(VS, t), vsum, -0.5, None, ALU.mult).then_inc(s("v"), 1)
                        dve.wait_ge(s("v"), t + 1)
                    dve.wait_ge(s("x"), (t + z) + 1)

                masks(0, 0)

                def body(b):
                    for k in (0, 1):
                        t = b + k
                        if not isinstance(t, int) or t + 1 < NSEQ:
                            masks(t + 1, 1 - k)
                        step(t)
                pairs_ends(dve, body)
            iterate(1)
            iterate(2)

            dve.wait_ge(S["d0_xb"], NSEQ)

            def refine(b):
                for k in (0, 1):
                    t = b + k
                    dve.wait_ge(S["e_2"], t + 1)
                    need(dve, S["e_x"], t - 1)
                    dve.tensor_tensor(ot[:, k].rearrange("p (j d) -> p j d", j=TILES),
                                      PS[:, 2 + k, :].rearrange("p (j d) -> p j d", j=TILES), rows(wl("iwrow")), ALU.mult)\
                        .then_inc(S["e_t"], 1)
                    dve.wait_ge(S["e_t"], t + 1)
                    dve.tensor_tensor(tiles(X, t), tiles(X, t), ot[:, k].rearrange("p (j d) -> p j d", j=TILES), ALU.add)\
                        .then_inc(S["e_x"], 1)
            pairs(dve, refine)

        @block.scalar
        def _(act):
            def root(count):
                act.wait_ge(S["ln_var"], count)
                act.activation(SD[:, :], v1, ACT.Sqrt).then_inc(S["ln_sd"], 1)

            act.dma_start(WE[:, 0:FIRST_N], early[:, 0:FIRST_N]).then_inc(S["w_first"], 16)
            for h in (0, 1):
                act.wait_ge(S["var_half"], h + 1)
                act.activation(SD[:, h * NT // 2:(h + 1) * NT // 2], v1[:, h * NT // 2:(h + 1) * NT // 2], ACT.Sqrt)\
                    .then_inc(S["sd_half"], 1)

            def a1(b):
                for k in (0, 1):
                    t = b + k
                    act.wait_ge(S["a1_tr"], t + 1)
                    need(act, S["a1_mm"], 4 * (t - 1))
                    act.activation(xT[:, k], PS[:, k, :], ACT.Copy).then_inc(S["a1_xt"], 1)
                for k in (0, 1):
                    for j in range(TILES):
                        n = 4 * (b + k) + j
                        act.wait_ge(S["a1_ev"], n + 1)
                        for c in (0, 1):
                            need(act, S["a1_sq"], 2 * n + c - 3)
                            act.activation(junk[:, 2 * (j % 2) + c], QKV[:, bass.ds(n, 1), c, 0:P].rearrange("p a d -> p (a d)"),
                                           ACT.Square, accum_out=ssq[:, bass.ds(n, 1), c]).then_inc(S["a1_sq"], 1)

            def norms(part):
                act.wait_ge(S["a1_sq"], 2 * part.stop)
                act.activation(ssq[:, part], ssq[:, part], ACT.Sqrt).then_inc(S["a1_nrm"], 1)

            a1(0)
            with act.Fori(1, NSEQ // 2 - 1) as pair:
                a1(pair * 2)
            norms(MOST)
            a1(NSEQ - 2)
            norms(LAST)
            act.wait_ge(S["w_early"], 16)

            def a2(b):
                for k in (0, 1):
                    t = b + k
                    act.wait_ge(S["a2_tq"], t + 1)
                    need(act, S["a2_s"], 4 * (t - 1))
                    act.activation(qT[:, k], PS[:, 0, :], ACT.Copy).then_inc(S["a2_qT"], 1)
                    act.wait_ge(S["a2_tk"], t + 1)
                    act.activation(kT[:, k], PS[:, 1, :], ACT.Copy).then_inc(S["a2_kT"], 1)
                    need(act, S["a2_o"], t - 1)
                    for c in range(TILES):
                        act.wait_ge(S["a2_s"], 4 * t + c + 1)
                        act.activation(E[:, k, SEQ * c:SEQ * (c + 1)], PS[:, 2 + c, :], ACT.Exp).then_inc(S["a2_E"], 1)
                for k in (0, 1):
                    t = b + k
                    act.wait_ge(S["a2_to"], t + 1)
                    need(act, S["a2_w1"], t - 1)
                    act.activation(oT[:, k], PS[:, 0, :], ACT.Copy).then_inc(S["a2_oT"], 1)
                for k in (0, 1):
                    t = b + k
                    need(act, S["a2_w3"], t - 1)
                    for c in range(HC):
                        act.wait_ge(S["a2_w2"], 4 * t + c + 1)
                        act.activation(h2[:, k, SEQ * c:SEQ * (c + 1)], PS[:, 2 + c, :], ACT.Relu,
                                       bias=we("b2")[:, c:c + 1]).then_inc(S["a2_h2"], 1)
            pairs(act, a2)
            root(1)

            act.wait_ge(S["ln_rs"], 2)

            def b_(b):
                for k in (0, 1):
                    t = b + k
                    act.wait_ge(S["b_tr"], t + 1)
                    need(act, S["b_xk"], t - 1)
                    act.activation(b_xT[:, k, 1:SEQ + 1], PS[:, k, :], ACT.Copy).then_inc(S["b_xT"], 1)
                    act.wait_ge(S["b_xT"], t + 1)
                    act.activation(b_tr[:, k], b_xT[:, k, 0:SEQ], ACT.Copy, scale=om_r)
                    act.activation(b_tk[:, k], b_xT[:, k, 0:SEQ], ACT.Copy, scale=om_k).then_inc(S["b_tk"], 1)
                for k in (0, 1):
                    t = b + k
                    act.wait_ge(S["b_r"], t + 1)
                    need(act, S["b_ot"], t - 1)
                    act.activation(b_rs[:, k], PS[:, 2 + k, :], ACT.Sigmoid).then_inc(S["b_rs"], 1)
                    act.wait_ge(S["b_k"], t + 1)
                    need(act, S["b_ka"], t - 1)
                    act.activation(b_kr[:, k], PS[:, 4 + k, :], ACT.Relu).then_inc(S["b_kr"], 1)
            pairs(act, b_)
            root(2)
            root(3)

            act.wait_ge(S["ln_rs"], 3)

            def x1(t):
                for j in range(TILES):
                    n = t * TILES + j
                    act.activation(XP[:, bass.ds(n, 1), :].rearrange("p a d -> p (a d)"),
                                   X[:, bass.ds(n, 1), :].rearrange("p a d -> p (a d)"), ACT.Identity,
                                   scale=RS[:, 0, bass.ds(n, 1)], bias=nmr[:, bass.ds(n, 1)]).then_inc(S["c1_x1"], 1)

            def project(t, k):
                act.wait_ge(S["c1_tr"], t + 1)
                need(act, S["c1_q"], t - 1)
                act.activation(c_hT[:, k], PS[:, 0, :], ACT.Identity, scale=we("ln1_g"), bias=we("ln1_b")).then_inc(S["c1_hT"], 1)
                need(act, S["c1_red"], 4 * (t - 1))
                for j in range(TILES):
                    act.wait_ge(S["c1_mm"], 4 * t + j + 1)
                    act.activation(tok[:, k, j], PS[:, (1 + j) % 2, 0:384], ACT.Copy).then_inc(S["c1_tok"], 1)
                act.wait_ge(S["c1_q"], t + 1)
                need(act, S["c1_yin"], t - 1)
                act.activation(c_qT[:, k], PS[:, 1, :], ACT.Copy).then_inc(S["c1_qT"], 1)

            def turned(t, k):
                act.wait_ge(S["c1_ty"], t + 1)
                need(act, S["c1_wo"], t - 1)
                act.activation(c_yT[:, k], PS[:, 0, :], ACT.Copy).then_inc(S["c1_yT"], 1)

            x1(0)
            x1(1)
            project(0, 0)

            def c1(b):
                for k in (0, 1):
                    t = b + k
                    if not isinstance(t, int) or t + 1 < NSEQ:
                        project(t + 1, 1 - k)
                    if not isinstance(t, int) or t > 0:
                        turned(t - 1, 1 - k)
                    if not isinstance(b, int) or t + 2 < NSEQ:
                        x1(t + 2)
            pairs_ends(act, c1)
            turned(NSEQ - 1, 1)
            root(4)

            act.wait_ge(S["w_late"], 16)
            act.activation(swc, wl("shw"), ACT.Tanh, scale=0.5).then_inc(S["k_sw"], 1)

            def c3(b):
                for k in (0, 1):
                    t = b + k
                    act.wait_ge(S["c3_tr"], t + 1)
                    need(act, S["c3_h"], t - 1)
                    need(act, S["c3_w1"], 12 * b - 4 + 4 * k)
                    act.activation(hTr[:, k, 0], PS[:, k, :], ACT.Identity, scale=we("ln2_g"), bias=we("ln2_b"))
                    act.activation(d_hT[:, k], PS[:, k, :], ACT.Identity, scale=we("ln2_g"), bias=we("ln2_b"))\
                        .then_inc(S["c3_hT"], 1)
                for lev in range(LEVELS):
                    for k in (0, 1):
                        need(act, S["c3_w2"], 3 * b + 2 * lev + k - 1)
                        for c in range(HC):
                            act.wait_ge(S["c3_w1"], 12 * b + 8 * lev + 4 * k + c + 1)
                            bias = we("cb1")[:, 4 * lev + c:4 * lev + c + 1]
                            if lev < LEVELS - 1:
                                act.activation(Gr[:, k, 0, SEQ * c:SEQ * (c + 1)], PS[:, 2 + c, :], ACT.Gelu_apprx_tanh, bias=bias)
                            act.activation(d_G[:, k, SEQ * c:SEQ * (c + 1)], PS[:, 2 + c, :], ACT.Gelu_apprx_tanh, bias=bias)\
                                .then_inc(S["c3_g"], 1)
            pairs(act, c3)
            root(5)

            act.wait_ge(S["ln_rs"], 5)

            def d0(b):
                for k in (0, 1):
                    t = b + k
                    act.wait_ge(S["d0_tr"], t + 1)
                    act.activation(seq(XI, t), PS[:, k, :], ACT.Copy).then_inc(S["d0_xi"], 1)
                for k in (0, 1):
                    t = b + k
                    act.wait_ge(S["d0_r"], t + 1)
                    need(act, S["d0_l"], t - 1)
                    act.activation(e_rh[:, k], PS[:, 2 + k, :], ACT.Gelu, bias=wl("rb1")).then_inc(S["d0_rh"], 1)
            pairs(act, d0)
            act.wait_ge(S["d0_d"], NSEQ)
            act.activation(th, dd, ACT.Tanh, scale=0.5).then_inc(S["d0_th"], 1)

            def rows_out():
                def body(b):
                    for k in (0, 1):
                        t = b + k
                        act.wait_ge(S["d0_ot"], t + 1)
                        act.activation(OH[0:96, 1, bass.ds(t * SEQ, SEQ)], PS[0:96, 5 + 2 * k, 0:256].bitcast(BF16),
                                       ACT.Copy).then_inc(S["d0_oh2"], 1)
                pairs(act, body)

            def iterate(it):
                z = NSEQ * (it - 1)
                s = lambda n: S[f"d_{n}"]

                def hidden(t, k):
                    need(act, s("u"), U0[it] + NU[it] * (t - 1))
                    act.wait_ge(s("g"), 5 * (t + z) + 1)
                    act.activation(hs[0:96, k], PS[0:96, 0, :], ACT.Gelu, bias=wl("g1b")[0:96]).then_inc(s("ge"), 1)
                    for c in range(HC):
                        act.wait_ge(s("g"), 5 * (t + z) + c + 2)
                        need(act, s("hm"), 8 * ((t + z) - 1) + 2 * c + 2)
                        act.activation(hE[:, c], PS[:, (c + 1) % 2, :], ACT.Gelu, bias=wl("eb1")[:, c:c + 1]).then_inc(s("ge"), 1)

                def control(t):
                    for u, (part, e, bank) in enumerate(UNITS[it]):
                        act.wait_ge(s("u"), U0[it] + NU[it] * t + u + 1)
                        if part == "b":
                            if e == 0:
                                need(act, s("x"), (t + z))
                            act.activation(az[:, e], PS[:, bank, :], ACT.Abs)
                            act.activation(rz[:, e], PS[:, bank, :], ACT.Relu).then_inc(s("ev"), 1)
                            if e == 2:
                                act.wait_ge(s("ev"), U0[it] + NU[it] * t + u + 1)
                                act.activation(az, az, ACT.Exp, scale=-1.0).then_inc(s("ex"), 1)
                                act.wait_ge(s("ex"), (t + z) + 1)
                                act.activation(az, az, ACT.Ln, bias=1.0).then_inc(s("ln"), 1)
                        elif part == "h":
                            act.activation(hlt, PS[:, bank, :], ACT.Tanh, scale=0.5, bias=hb2h).then_inc(s("ev"), 1)
                        else:
                            act.activation((ta_ if part == "a" else tgt)[:, e], PS[:, bank, :], ACT.Tanh, scale=0.5)\
                                .then_inc(s("ev"), 1)

                hidden(0, 0)
                if it == 1:
                    rows_out()

                def body(b):
                    for k in (0, 1):
                        t = b + k
                        if not isinstance(t, int) or t + 1 < NSEQ:
                            hidden(t + 1, 1 - k)
                        control(t)
                pairs_ends(act, body)
            act.wait_ge(S["k_sets"], 1)
            act.activation(hb2h, wl("hb2"), ACT.Copy, scale=0.5).then_inc(S["k_sw"], 1)
            act.wait_ge(S["k_sw"], 2)
            act.wait_ge(S["d0_xa"], NSEQ)
            iterate(1)
            iterate(2)

            act.wait_ge(S["d_hm"], 16 * NSEQ)

            def refine(b):
                for k in (0, 1):
                    t = b + k
                    need(act, S["e_2"], t - 1)
                    for c in (0, 1):
                        act.wait_ge(S["e_1"], 2 * t + c + 1)
                        act.activation(rf[:, k, SEQ * c:SEQ * (c + 1)], PS[:, c, :], ACT.Gelu, bias=wl("fb1")[:, c:c + 1])\
                            .then_inc(S["e_g"], 1)
            pairs(act, refine)

        @block.tensor
        def _(pe):
            def turn(bank, src, k, eye):
                for j in range(TILES):
                    last = pe.transpose(PS[:, bank, P * j:P * (j + 1)], src[:, k, j], eye)
                return last

            pe.wait_ge(S["w_first"], 16)

            def a1(b):
                for k in (0, 1):
                    t = b + k
                    pe.wait_ge(S["a1_xn"], t + 1)
                    need(pe, S["a1_xt"], t - 1)
                    turn(k, xn, k, ident).then_inc(S["a1_tr"], 1)
                for k in (0, 1):
                    t = b + k
                    pe.wait_ge(S["a1_xt"], t + 1)
                    for j in range(TILES):
                        need(pe, S["a1_ev"], 4 * (t - 1) + j + 1)
                        pe.matmul(PS[:, 2 + j, 0:384], xT[:, k, P * j:P * (j + 1)], we("wqkv"), start=True, stop=True)\
                            .then_inc(S["a1_mm"], 1)
            pairs(pe, a1)

            def qk_turn(t, k):
                pe.wait_ge(S["a2_qk"], 2 * t + 2)
                if k == 0:
                    need(pe, S["a2_x"], t)
                    need(pe, S["a2_h1"], t)
                else:
                    pe.wait_ge(S["a2_qT"], t)
                    pe.wait_ge(S["a2_kT"], t)
                turn(0, qn, k, ident).then_inc(S["a2_tq"], 1)
                turn(1, kn, k, ident).then_inc(S["a2_tk"], 1)

            def scores(t, k):
                pe.wait_ge(S["a2_qT"], t + 1)
                pe.wait_ge(S["a2_kT"], t + 1)
                for c in range(TILES):
                    if k == 0:
                        need(pe, S["a2_h2"], 4 * (t - 1) + c + 1)
                    else:
                        pe.wait_ge(S["a2_E"], 4 * (t - 1) + c + 1)
                    pe.matmul(PS[:, 2 + c, :], kT[:, k, P * c:P * (c + 1)], qT[:, k], start=True, stop=True)\
                        .then_inc(S["a2_s"], 1)

            def values(t, k):
                pe.wait_ge(S["a2_E"], 4 * t + 4)
                need(pe, S["a2_on"], t)
                for j in range(TILES):
                    for c in range(TILES):
                        last = pe.matmul(PS[:, 6 + j // 2, 129 * (j % 2):129 * (j % 2) + 129],
                                         E[:, k, SEQ * c + P * j:SEQ * c + P * (j + 1)],
                                         QKV[:, bass.ds(t * TILES + c, 1), 2, 0:129].rearrange("p a d -> p (a d)"),
                                         start=c == 0, stop=c == TILES - 1)
                last.then_inc(S["a2_o"], 1)

            def o_turn(t, k):
                pe.wait_ge(S["a2_on"], t + 1)
                if k == 0:
                    pe.wait_ge(S["a2_qT"], t + 2)
                else:
                    pe.wait_ge(S["a2_oT"], t)
                turn(0, on, k, ident).then_inc(S["a2_to"], 1)

            def mlp1(t, k):
                pe.wait_ge(S["a2_oT"], t + 1)
                if k == 0:
                    pe.wait_ge(S["a2_kT"], t + 2)
                else:
                    pe.wait_ge(S["a2_h1"], t)
                pe.matmul(PS[:, 1, :], we("w1"), oT[:, k], start=True, stop=True).then_inc(S["a2_w1"], 1)

            def mlp2(t, k):
                pe.wait_ge(S["a2_h1"], t + 1)
                for c in range(HC):
                    if k == 0:
                        pe.wait_ge(S["a2_E"], 4 * (t + 1) + c + 1)
                    else:
                        pe.wait_ge(S["a2_h2"], 4 * (t - 1) + c + 1)
                    pe.matmul(PS[:, 2 + c, :], we("w2")[:, P * c:P * (c + 1)], h1[:, k], start=True, stop=True)\
                        .then_inc(S["a2_w2"], 1)

            def mlp3(t, k):
                pe.wait_ge(S["a2_h2"], 4 * t + 4)
                if k == 0:
                    pe.wait_ge(S["a2_oT"], t + 2)
                else:
                    pe.wait_ge(S["a2_x"], t)
                for j in range(TILES):
                    for c in range(HC):
                        last = pe.matmul(PS[:, 0, P * j:P * (j + 1)], h2[:, k, SEQ * c + P * j:SEQ * c + P * (j + 1)],
                                         we("w3")[:, P * c:P * (c + 1)], start=c == 0, stop=c == HC - 1)
                last.then_inc(S["a2_w3"], 1)

            def a2(b):
                qk_turn(b, 0)
                scores(b, 0)
                qk_turn(b + 1, 1)
                values(b, 0)
                scores(b + 1, 1)
                o_turn(b, 0)
                values(b + 1, 1)
                mlp1(b, 0)
                o_turn(b + 1, 1)
                mlp2(b, 0)
                mlp1(b + 1, 1)
                mlp3(b, 0)
                mlp2(b + 1, 1)
                mlp3(b + 1, 1)
            pe.wait_ge(S["a1_rn"], 1)
            pe.wait_ge(S["w_early"], 16)
            pairs(pe, a2)

            pe.wait_ge(S["ln_rs"], 2)

            def b_(b):
                for k in (0, 1):
                    t = b + k
                    pe.wait_ge(S["b_xn"], t + 1)
                    need(pe, S["b_xT"], t - 1)
                    turn(k, b_xn, k, ident).then_inc(S["b_tr"], 1)
                for k in (0, 1):
                    t = b + k
                    pe.wait_ge(S["b_xr"], t + 1)
                    need(pe, S["b_rs"], t - 1)
                    for j in range(TILES):
                        last = pe.matmul(PS[:, 2 + k, P * j:P * (j + 1)], b_xr[:, k, P * j:P * (j + 1)], we("wr"),
                                         start=True, stop=True)
                    last.then_inc(S["b_r"], 1)
                    pe.wait_ge(S["b_xk"], t + 1)
                    need(pe, S["b_kr"], t - 1)
                    pe.matmul(PS[:, 4 + k, :], we("wk"), b_xk[:, k], start=True, stop=True).then_inc(S["b_k"], 1)
                for k in (0, 1):
                    t = b + k
                    pe.wait_ge(S["b_ka"], t + 1)
                    need(pe, S["b_ot"], t - 1)
                    for j in range(TILES):
                        last = pe.matmul(PS[:, 6 + k, P * j:P * (j + 1)], b_ka[:, k, P * j:P * (j + 1)], we("wv"),
                                         start=True, stop=True)
                    last.then_inc(S["b_o"], 1)
            pairs(pe, b_)

            pe.wait_ge(S["ln_rs"], 3)

            def project(t, k):
                pe.wait_ge(S["c1_hn"], t + 1)
                need(pe, S["c1_tok"], 4 * t)
                need(pe, S["c1_yT"], t - 2)
                turn(0, c_hn, k, ident).then_inc(S["c1_tr"], 1)
                pe.wait_ge(S["c1_hT"], t + 1)
                need(pe, S["c1_qT"], t)
                for j in range(TILES):
                    if j >= 2:
                        pe.wait_ge(S["c1_tok"], 4 * t + j - 1)
                    pe.matmul(PS[:, (1 + j) % 2, 0:384], c_hT[:, k, P * j:P * (j + 1)], we("lqkv"), start=True, stop=True)\
                        .then_inc(S["c1_mm"], 1)
                pe.wait_ge(S["c1_tok"], 4 * t + 3)
                pe.matmul(PS[:, 1, :], we("lqkv")[:, 0:P], c_hT[:, k], start=True, stop=True).then_inc(S["c1_q"], 1)
                pe.wait_ge(S["c1_tok"], 4 * t + 4)
                need(pe, S["c1_M"], t)
                need(pe, S["c1_xp"], t - 2)
                for m in range(3):
                    for c in range(m + 1):
                        last = pe.matmul(PS[:, 2, P * m:P * (m + 1)], tok[:, k, c, P:2 * P], tok[:, k, c, 2 * P:3 * P],
                                         start=c == 0, stop=c == m)
                last.then_inc(S["c1_m"], 1)

            def attend(t, k):
                pe.wait_ge(S["c1_M"], t + 1)
                pe.wait_ge(S["c1_qT"], t + 1)
                need(pe, S["c1_y"], t)
                for c in range(1, TILES):
                    last = pe.matmul(PS[:, 3, P * (c - 1):P * c], c_qT[:, k, P * c:P * (c + 1)], Mbd[:, k, c - 1],
                                     start=True, stop=True)
                last.then_inc(S["c1_yin"], 1)
                for c in range(TILES):
                    pe.wait_ge(S["c1_kv"], 4 * t + c + 1)
                    need(pe, S["c1_qm"], 4 * t + c - 1)
                    for h in (0, 1):
                        last = pe.matmul(PS[:, 4 + 2 * (c % 2) + h, :], we("tril"), kv[:, c % 2, SEQ * h:SEQ * (h + 1)],
                                         start=True, stop=True)
                    last.then_inc(S["c1_in"], 1)

            def finish(t, k, ahead):
                pe.wait_ge(S["c1_y"], t + 1)
                pe.wait_ge(S["c1_tok"], 4 * ahead)
                turn(0, c_y, k, ident).then_inc(S["c1_ty"], 1)
                pe.wait_ge(S["c1_yT"], t + 1)
                pe.wait_ge(S["c1_M"], ahead)
                need(pe, S["c1_xp"], t)
                for j in range(TILES):
                    last = pe.matmul(PS[:, 2, P * j:P * (j + 1)], c_yT[:, k, P * j:P * (j + 1)], we("lwo"), start=True, stop=True)
                last.then_inc(S["c1_wo"], 1)

            project(0, 0)

            def c1(b):
                for k in (0, 1):
                    t = b + k
                    if not isinstance(t, int) or t + 1 < NSEQ:
                        project(t + 1, 1 - k)
                    attend(t, k)
                    if not isinstance(t, int) or t > 0:
                        finish(t - 1, 1 - k, min(t + 2, NSEQ) if isinstance(t, int) else t + 2)
            pairs_ends(pe, c1)
            finish(NSEQ - 1, 1, NSEQ)

            pe.wait_ge(S["ln_rs"], 4)
            pe.wait_ge(S["c3_wh"], 2)

            def c3(b):
                for k in (0, 1):
                    t = b + k
                    pe.wait_ge(S["c3_xn"], t + 1)
                    need(pe, S["c3_hT"], t - 1)
                    turn(k, d_xn, k, ident).then_inc(S["c3_tr"], 1)
                for lev in range(LEVELS):
                    for k in (0, 1):
                        if lev == 0:
                            pe.wait_ge(S["c3_h"], b + k + 1)
                        else:
                            pe.wait_ge(S["c3_w2e"], 3 * b + 2 * (lev - 1) + k + 1)
                        for c in range(HC):
                            need(pe, S["c3_g"], 12 * b + 8 * lev + 4 * k + c - 3)
                            at = 512 * lev + P * c
                            for n, (pw, px) in enumerate(PASSES):
                                last = pe.matmul(PS[:, 2 + c, :], CWr[:, pw, at:at + P], hTr[:, k, px],
                                                 start=n == 0, stop=n == 2)
                            last.then_inc(S["c3_w1"], 1)
                    for k in (0, 1):
                        pe.wait_ge(S["c3_g"], 12 * b + 8 * lev + 4 * k + 4)
                        need(pe, S["c3_w2e"], 3 * b + 2 * lev + k - 1)
                        w2 = we("cw2")[:, 512 * lev:512 * (lev + 1)]
                        if lev < LEVELS - 1:
                            for c in range(HC):
                                pe.wait_ge(S["c3_lo"], 8 * b + 8 * lev + 4 * k + c + 1)
                                at = LEVELS * 512 + 512 * lev + P * c
                                for n, (pw, px) in enumerate(PASSES):
                                    last = pe.matmul(PS[:, 6 + k, :], CWr[:, pw, at:at + P], Gr[:, k, px, SEQ * c:SEQ * (c + 1)],
                                                     start=c + n == 0, stop=c == HC - 1 and n == 2)
                        else:
                            for j in range(TILES):
                                for c in range(HC):
                                    last = pe.matmul(PS[:, 6 + k, P * j:P * (j + 1)],
                                                     d_G[:, k, SEQ * c + P * j:SEQ * c + P * (j + 1)],
                                                     w2[:, P * c:P * (c + 1)], start=c == 0, stop=c == HC - 1)
                        last.then_inc(S["c3_w2"], 1)
            pairs(pe, c3)

            pe.wait_ge(S["ln_rs"], 5)
            pe.wait_ge(S["w_late"], 16)
            pe.wait_ge(S["k_sets"], 1)

            def d0(b):
                for k in (0, 1):
                    t = b + k
                    pe.wait_ge(S["d0_xn"], t + 1)
                    need(pe, S["d0_xi"], t - 1)
                    turn(k, e_xn, k, wl("lident")).then_inc(S["d0_tr"], 1)
                for k in (0, 1):
                    t = b + k
                    pe.wait_ge(S["d0_xi"], t + 1)
                    need(pe, S["d0_rh"], t - 1)
                    pe.matmul(PS[:, 2 + k, :], wl("rw1"), seq(XI, t), start=True, stop=True).then_inc(S["d0_r"], 1)
                for k in (0, 1):
                    t = b + k
                    pe.wait_ge(S["d0_rh"], t + 1)
                    need(pe, S["d0_lg"], t - 1)
                    for j in range(TILES):
                        last = pe.matmul(PS[:, 4 + k, 8 * j:8 * j + 8], e_rh[:, k, P * j:P * (j + 1)], wl("rw2"), start=True, stop=True)
                    last.then_inc(S["d0_l"], 1)
            pairs(pe, d0)

            def rows_turned():
                pe.wait_ge(S["d0_cw"], 5)
                for t in range(NSEQ):
                    need(pe, S["d0_oh1"], t - 1)
                    need(pe, S["d0_oh2"], t - 1)
                    for e in (0, 1):
                        for j in range(TILES):
                            last = pe.transpose(PS[0:96, 4 + 2 * (t % 2) + e, 64 * j:64 * (j + 1)].bitcast(BF16),
                                                oht[:, e, t * TILES + j].rearrange("p g r -> p (g r)"), eyeb)
                    last.then_inc(S["d0_ot"], 1)
                pe.wait_ge(S["d0_oh1"], NSEQ)
                pe.wait_ge(S["d0_oh2"], NSEQ)

            pe.wait_ge(S["d_wh"], 2)

            def iterate(it):
                z = NSEQ * (it - 1)
                s = lambda n: S[f"d_{n}"]

                def hidden(t, t_par):
                    pe.wait_ge(s("xs"), (t + z) + 1)
                    for g in range(1 + HC):
                        need(pe, s("ge"), 5 * (t + z) + g - 1 if g >= 2 else 5 * (t + z))
                        m = 96 if g == 0 else P
                        bank = g % 2
                        n = 0
                        for i, name in enumerate((("g1x", "g1v") if g == 0 else ("ew1x", "ew1v"))[:it]):
                            for pw, px in PASSES:
                                lhs = w1(name, pw) if g == 0 else w1(name, pw)[:, P * (g - 1):P * g]
                                last = pe.matmul(PS[0:m, bank, :], lhs, XVS[:, t_par, i, px], start=n == 0, stop=n == 3 * it - 1)
                                n += 1
                        last.then_inc(s("g"), 1)

                def mask(t, c):
                    need(pe, s("hm"), 8 * (t + z) + 2 * c)
                    if c == 0:
                        need(pe, s("U"), 2 * (t + z - 1))
                    for e in (0, 1):
                        last = pe.matmul(PS[:, 2 + e, :], esel[0:96, P * c:P * (c + 1)], OH[0:96, e, bass.ds(t * SEQ, SEQ)],
                                         start=True, stop=True)
                    last.then_inc(s("m"), 1)

                def weights(t, more):
                    pe.wait_ge(s("hm"), 8 * (t + z) + (16 if more else 8))
                    for e in (0, 1):
                        last = pe.matmul(PS[:, 2 + e, :], csel[0:96], OH[0:96, e, bass.ds(t * SEQ, SEQ)], start=True, stop=True)
                    last.then_inc(s("C"), 1)

                def unit(t, k, u):
                    part, e, bank = UNITS[it][u]
                    before = [v for v in range(NU[it]) if UNITS[it][v][2] == bank and v < u]
                    later = [v for v in range(NU[it]) if UNITS[it][v][2] == bank]
                    need(pe, s("ev"), U0[it] + NU[it] * t + before[-1] + 1 if before else U0[it] + NU[it] * (t - 1) + later[-1] + 1)
                    if part == "h":
                        pe.matmul(PS[:, bank, :], wl("hw2")[0:96], hs[0:96, k], start=True, stop=True).then_inc(s("u"), 1)
                        return
                    col = P * "abg".index(part)
                    pe.matmul(PS[:, bank, :], bias2[0:96, 0 if e else 1, col:col + P],
                              OH[0:96, max(e - 1, 0), bass.ds(t * SEQ, SEQ)], start=True, stop=False)
                    if e == 0:
                        pe.matmul(PS[:, bank, :], wl("sw2")[0:96, col:col + P], hs[0:96, k], start=False, stop=True)\
                            .then_inc(s("u"), 1)
                        return
                    for c in range(HC):
                        last = pe.matmul(PS[:, bank, :], wl("ew2")[:, 384 * c + col:384 * c + col + P],
                                         hM[:, k, e - 1, SEQ * c:SEQ * (c + 1)], start=False, stop=c == HC - 1)
                    last.then_inc(s("u"), 1)

                hidden(0, 0)
                if it == 1:
                    rows_turned()
                else:
                    pe.wait_ge(s("ev"), U0[it])
                    pe.wait_ge(s("U"), 2 * NSEQ)
                for c in range(HC):
                    mask(0, c)

                def body(b):
                    for k in (0, 1):
                        t = b + k
                        more = not isinstance(t, int) or t + 1 < NSEQ
                        if more:
                            hidden(t + 1, 1 - k)
                        pe.wait_ge(s("ge"), 5 * (t + z) + 1)
                        for u in range(NU[it]):
                            if u == 1:
                                pe.wait_ge(s("hm"), 8 * (t + z) + 8)
                            unit(t, k, u)
                            if more and u < HC:
                                mask(t + 1, u)
                            if u == HC:
                                weights(t, more)
                pairs_ends(pe, body)
            iterate(1)
            iterate(2)


            def refine(b):
                for k in (0, 1):
                    t = b + k
                    pe.wait_ge(S["d_x"], NSEQ + t + 1)
                    for c in (0, 1):
                        need(pe, S["e_g"], 2 * t + c - 1)
                        pe.matmul(PS[:, c, :], wl("fw1")[:, P * c:P * (c + 1)], seq(XI, t), start=True, stop=True)\
                            .then_inc(S["e_1"], 1)
                for k in (0, 1):
                    t = b + k
                    pe.wait_ge(S["e_g"], 2 * t + 2)
                    if isinstance(t, int):
                        pe.wait_ge(S["d_U"], 4 * NSEQ)
                    need(pe, S["e_t"], t - 1)
                    for j in range(TILES):
                        for c in (0, 1):
                            last = pe.matmul(PS[:, 2 + k, P * j:P * (j + 1)], rf[:, k, SEQ * c + P * j:SEQ * c + P * (j + 1)],
                                             wl("fw2")[:, P * c:P * (c + 1)], start=c == 0, stop=c == 1)
                    last.then_inc(S["e_2"], 1)
            pairs(pe, refine)


def pack_early(i):
    a = np.zeros((P, EARLY_N), np.float32)

    def put(name, v):
        s, z = EARLY_AT[name]
        v = np.asarray(v).reshape(-1, z - s) if np.ndim(v) != 1 or z - s > 1 else np.asarray(v)[:, None]
        a[:v.shape[0] if v.shape[0] > 1 else P, s:z] = v

    put("ident", np.eye(P, dtype=np.float32))
    put("tril", np.triu(np.ones((P, P), np.float32)))
    put("blockdiag", np.kron(np.eye(HEADS, dtype=np.float32), np.ones((HD, HD), np.float32)))
    put("wqkv", np.concatenate([i["L0_attn_Wq"].T, i["L0_attn_Wk"].T, i["L0_attn_Wv"].T], 1))
    put("bqkv", np.concatenate([i["L0_attn_bq"], i["L0_attn_bk"], i["L0_attn_bv"]])[None])
    put("w1", i["L0_attn_W1"].T)
    put("b1", i["L0_attn_b1"])
    put("w2", i["L0_attn_W2"].T)
    put("b2", i["L0_attn_b2"].reshape(HC, P).T)
    put("w3", i["L0_attn_W3"].T.reshape(HC, P, P).transpose(1, 0, 2).reshape(P, 512))
    put("b3", i["L0_attn_b3"][None])
    put("wr", i["L0_ffn_W_r"].T)
    put("wk", i["L0_ffn_W_k"].T)
    put("wv", i["L0_ffn_W_v"].T)
    for n in ("mu_r", "mu_k"):
        put(n, i["L0_ffn_" + n])
    for n in ("ln1_g", "ln1_b", "ln2_g", "ln2_b"):
        put(n, i["L1_attn_" + n])
    put("lqkv", np.concatenate([i["L1_attn_wq"], i["L1_attn_wk"], i["L1_attn_wv"]], 1))
    put("lwo", i["L1_attn_wo"])
    put("cw1", i["L1_attn_cms_w1"].transpose(1, 0, 2).reshape(P, LEVELS * 512))
    put("cb1", i["L1_attn_cms_b1"].reshape(LEVELS * HC, P).T)
    put("cw2", i["L1_attn_cms_w2"].reshape(LEVELS, HC, P, P).transpose(2, 0, 1, 3).reshape(P, LEVELS * 512))
    put("cb2", i["L1_attn_cms_b2"].T)
    put("cb2row", i["L1_attn_cms_b2"][LEVELS - 1][None])
    return a


def pack_late(i):
    a = np.zeros((P, LATE_N), np.float32)

    def put(name, v, row=0):
        s, z = LATE_AT[name]
        a[row:row + v.shape[0], s:s + v.shape[1]] = v

    f = {n[len("L1_ffn_"):]: v for n, v in i.items() if n.startswith("L1_ffn_")}
    everywhere = lambda v: np.broadcast_to(v, (P, v.shape[-1]))
    put("lident", np.eye(P, dtype=np.float32))
    put("iota", everywhere(np.arange(EXPERTS, dtype=np.float32)))
    put("g1x", np.concatenate([f["shared_w1"][:P], f["halt_w1"]], 1))
    put("g1v", f["shared_w1"][P:])
    put("g1b", np.concatenate([f["shared_b1"], f["halt_b1"]])[:, None])
    put("ew1x", f["expert_w1"][:, :P].transpose(1, 0, 2).reshape(P, 512))
    put("ew1v", f["expert_w1"][:, P:].transpose(1, 0, 2).reshape(P, 512))
    put("eb1", f["expert_b1"].reshape(HC, P).T)
    put("rw1", f["router_w1"])
    put("rb1", f["router_b1"][:, None])
    put("rw2", f["router_w2"])
    put("rb2", everywhere(f["router_b2"]))
    put("sw2", f["shared_w2"])
    put("hw2", np.broadcast_to(f["halt_w2"], (HHID, P)), EHID)
    put("hb2", np.broadcast_to(f["halt_b2"], (P, 1)))
    put("ew2", f["expert_w2"].reshape(HC, P, 384).transpose(1, 0, 2).reshape(P, 4 * 384))
    for g in (0, 32, 64):
        put("eb2", f["expert_b2"], g)
        put("sb2", np.broadcast_to(f["shared_b2"], (EXPERTS, 384)), g)
    put("mu", f["mu"][:, None])
    put("shw", np.broadcast_to(f["shared_weight"], (P, 1)))
    put("esel", np.kron(np.eye(EXPERTS, dtype=np.float32), np.ones((1, EHID), np.float32)))
    for g in (0, 32, 64):
        put("csel", np.ones((1, P), np.float32), g + EXPERTS)
    put("fw1", f["refine_w1"])
    put("fb1", f["refine_b1"].reshape(2, P).T)
    put("fw2", f["refine_w2"].reshape(2, P, P).transpose(1, 0, 2).reshape(P, 256))
    put("fb2row", everywhere(f["refine_b2"]))
    put("iwrow", everywhere(f["integration_weight"]))
    return a


def kernel(**inputs):
    import numpy as _np
    import concourse.bacc as _bacc
    from concourse.bass_utils import run_bass_kernel_spmd as _run

    i = {n: _np.asarray(v) for n, v in inputs.items()}
    arrays = {"x": i["L0_attn_x"].reshape(NSEQ * SEQ, P), "early": pack_early(i), "late": pack_late(i)}
    nc = _bacc.Bacc("TRN2", target_bir_lowering=False, num_devices=1)
    aps = [nc.dram_tensor(n, a.shape, F32, kind="ExternalInput").ap() for n, a in arrays.items()]
    out = nc.dram_tensor("out", (NSEQ * SEQ, P), F32, kind="ExternalOutput").ap()
    build(nc, *aps, out)
    r = _run(nc, [arrays], core_ids=[0])
    return r.results[0]["out"].reshape(NSEQ, SEQ, P)
```
